# Optimizing a Trainium2 kernel written in Bass

```python
import numpy as np
import jax
import jax.numpy as jnp

def _softmax(x, axis=-1):
    return jax.nn.softmax(x, axis=axis)

def _gelu(x):
    return jax.nn.gelu(x, approximate=True)

def _silu(x):
    return jax.nn.silu(x)

def _sigmoid(x):
    return jax.nn.sigmoid(x)

def _layernorm(x, axis=-1, eps=1e-05):
    m = jnp.mean(x, axis=axis, keepdims=True)
    v = jnp.var(x, axis=axis, keepdims=True)
    return (x - m) / jnp.sqrt(v + eps)

def _scatter_add(tgt, idx, src, axis=0):
    return tgt.at[idx].add(src)

def _segment_sum(src, seg, n):
    return jax.ops.segment_sum(src, seg, n)
kernel_name = 'mk_dlrm_tower_d1_rec_r8_f65d67'

def setup_inputs(seed: int=0):
    np.random.seed(seed)
    _w = jnp.asarray

    def _rec_inputs():
        import jax
        import jax.numpy as jnp
        _tk = jax.random.key(seed)
        dense_ctx = jax.random.normal(jax.random.fold_in(_tk, 190), (512, 16), jnp.float32)
        ids = jnp.stack([jax.random.randint(jax.random.fold_in(_tk, 200 + f), (512,), 0, v, jnp.int32) for f, v in enumerate([1000, 1000, 1250, 1000, 1250, 1250, 1250, 1000, 1000, 125000, 1000, 1250, 125000, 1000, 1000, 125000, 12500, 1250, 1250, 1000, 12500, 1250, 1250, 1000, 125000, 125000, 1000, 125000, 1250, 12500, 12500, 1000, 1000, 125000, 12500, 12500, 12500, 125000, 12500])], axis=1)
        tbl_0 = 0.05 * jax.random.normal(jax.random.fold_in(_tk, 500 + 0), (1000, 16), jnp.float32)
        tbl_1 = 0.05 * jax.random.normal(jax.random.fold_in(_tk, 500 + 1), (1000, 16), jnp.float32)
        tbl_2 = 0.05 * jax.random.normal(jax.random.fold_in(_tk, 500 + 2), (1250, 16), jnp.float32)
        tbl_3 = 0.05 * jax.random.normal(jax.random.fold_in(_tk, 500 + 3), (1000, 16), jnp.float32)
        tbl_4 = 0.05 * jax.random.normal(jax.random.fold_in(_tk, 500 + 4), (1250, 16), jnp.float32)
        tbl_5 = 0.05 * jax.random.normal(jax.random.fold_in(_tk, 500 + 5), (1250, 16), jnp.float32)
        tbl_6 = 0.05 * jax.random.normal(jax.random.fold_in(_tk, 500 + 6), (1250, 16), jnp.float32)
        tbl_7 = 0.05 * jax.random.normal(jax.random.fold_in(_tk, 500 + 7), (1000, 16), jnp.float32)
        tbl_8 = 0.05 * jax.random.normal(jax.random.fold_in(_tk, 500 + 8), (1000, 16), jnp.float32)
        tbl_9 = 0.05 * jax.random.normal(jax.random.fold_in(_tk, 500 + 9), (125000, 16), jnp.float32)
        tbl_10 = 0.05 * jax.random.normal(jax.random.fold_in(_tk, 500 + 10), (1000, 16), jnp.float32)
        tbl_11 = 0.05 * jax.random.normal(jax.random.fold_in(_tk, 500 + 11), (1250, 16), jnp.float32)
        tbl_12 = 0.05 * jax.random.normal(jax.random.fold_in(_tk, 500 + 12), (125000, 16), jnp.float32)
        tbl_13 = 0.05 * jax.random.normal(jax.random.fold_in(_tk, 500 + 13), (1000, 16), jnp.float32)
        tbl_14 = 0.05 * jax.random.normal(jax.random.fold_in(_tk, 500 + 14), (1000, 16), jnp.float32)
        tbl_15 = 0.05 * jax.random.normal(jax.random.fold_in(_tk, 500 + 15), (125000, 16), jnp.float32)
        tbl_16 = 0.05 * jax.random.normal(jax.random.fold_in(_tk, 500 + 16), (12500, 16), jnp.float32)
        tbl_17 = 0.05 * jax.random.normal(jax.random.fold_in(_tk, 500 + 17), (1250, 16), jnp.float32)
        tbl_18 = 0.05 * jax.random.normal(jax.random.fold_in(_tk, 500 + 18), (1250, 16), jnp.float32)
        tbl_19 = 0.05 * jax.random.normal(jax.random.fold_in(_tk, 500 + 19), (1000, 16), jnp.float32)
        tbl_20 = 0.05 * jax.random.normal(jax.random.fold_in(_tk, 500 + 20), (12500, 16), jnp.float32)
        tbl_21 = 0.05 * jax.random.normal(jax.random.fold_in(_tk, 500 + 21), (1250, 16), jnp.float32)
        tbl_22 = 0.05 * jax.random.normal(jax.random.fold_in(_tk, 500 + 22), (1250, 16), jnp.float32)
        tbl_23 = 0.05 * jax.random.normal(jax.random.fold_in(_tk, 500 + 23), (1000, 16), jnp.float32)
        tbl_24 = 0.05 * jax.random.normal(jax.random.fold_in(_tk, 500 + 24), (125000, 16), jnp.float32)
        tbl_25 = 0.05 * jax.random.normal(jax.random.fold_in(_tk, 500 + 25), (125000, 16), jnp.float32)
        tbl_26 = 0.05 * jax.random.normal(jax.random.fold_in(_tk, 500 + 26), (1000, 16), jnp.float32)
        tbl_27 = 0.05 * jax.random.normal(jax.random.fold_in(_tk, 500 + 27), (125000, 16), jnp.float32)
        tbl_28 = 0.05 * jax.random.normal(jax.random.fold_in(_tk, 500 + 28), (1250, 16), jnp.float32)
        tbl_29 = 0.05 * jax.random.normal(jax.random.fold_in(_tk, 500 + 29), (12500, 16), jnp.float32)
        tbl_30 = 0.05 * jax.random.normal(jax.random.fold_in(_tk, 500 + 30), (12500, 16), jnp.float32)
        tbl_31 = 0.05 * jax.random.normal(jax.random.fold_in(_tk, 500 + 31), (1000, 16), jnp.float32)
        tbl_32 = 0.05 * jax.random.normal(jax.random.fold_in(_tk, 500 + 32), (1000, 16), jnp.float32)
        tbl_33 = 0.05 * jax.random.normal(jax.random.fold_in(_tk, 500 + 33), (125000, 16), jnp.float32)
        tbl_34 = 0.05 * jax.random.normal(jax.random.fold_in(_tk, 500 + 34), (12500, 16), jnp.float32)
        tbl_35 = 0.05 * jax.random.normal(jax.random.fold_in(_tk, 500 + 35), (12500, 16), jnp.float32)
        tbl_36 = 0.05 * jax.random.normal(jax.random.fold_in(_tk, 500 + 36), (12500, 16), jnp.float32)
        tbl_37 = 0.05 * jax.random.normal(jax.random.fold_in(_tk, 500 + 37), (125000, 16), jnp.float32)
        tbl_38 = 0.05 * jax.random.normal(jax.random.fold_in(_tk, 500 + 38), (12500, 16), jnp.float32)
        _rk = jax.random.fold_in(_tk, 7)
        W_top1 = 0.0606339 * jax.random.normal(jax.random.fold_in(_tk, 801), (272, 512), jnp.float32)
        W_top2 = 0.0441942 * jax.random.normal(jax.random.fold_in(_tk, 802), (512, 256), jnp.float32)
        W_top3 = 0.0625 * jax.random.normal(jax.random.fold_in(_tk, 803), (256, 1), jnp.float32)
        b_top1 = jnp.zeros((512,), jnp.float32)
        b_top2 = jnp.zeros((256,), jnp.float32)
        return (dense_ctx, ids, tbl_0, tbl_1, tbl_2, tbl_3, tbl_4, tbl_5, tbl_6, tbl_7, tbl_8, tbl_9, tbl_10, tbl_11, tbl_12, tbl_13, tbl_14, tbl_15, tbl_16, tbl_17, tbl_18, tbl_19, tbl_20, tbl_21, tbl_22, tbl_23, tbl_24, tbl_25, tbl_26, tbl_27, tbl_28, tbl_29, tbl_30, tbl_31, tbl_32, tbl_33, tbl_34, tbl_35, tbl_36, tbl_37, tbl_38, W_top1, b_top1, W_top2, b_top2, W_top3)
    dense_ctx, ids, tbl_0, tbl_1, tbl_2, tbl_3, tbl_4, tbl_5, tbl_6, tbl_7, tbl_8, tbl_9, tbl_10, tbl_11, tbl_12, tbl_13, tbl_14, tbl_15, tbl_16, tbl_17, tbl_18, tbl_19, tbl_20, tbl_21, tbl_22, tbl_23, tbl_24, tbl_25, tbl_26, tbl_27, tbl_28, tbl_29, tbl_30, tbl_31, tbl_32, tbl_33, tbl_34, tbl_35, tbl_36, tbl_37, tbl_38, W_top1, b_top1, W_top2, b_top2, W_top3 = _rec_inputs()

    def _L0_rec_setup():
        import jax, jax.numpy as jnp
        import numpy as np
        LAYER_SIZES = [128, 128, 128]
        F0 = 39
        D = 16
        B = 256
        key = jax.random.key(seed)
        ks = jax.random.split(key, 4)
        field_nums = [F0, LAYER_SIZES[0] // 2, LAYER_SIZES[1] // 2]
        x = jax.random.normal(ks[0], (B, F0, D), dtype=jnp.float32)
        W0 = jax.random.normal(ks[1], (F0 * field_nums[0], LAYER_SIZES[0]), dtype=jnp.float32) * 0.05
        W1 = jax.random.normal(ks[2], (F0 * field_nums[1], LAYER_SIZES[1]), dtype=jnp.float32) * 0.05
        W2 = jax.random.normal(ks[3], (F0 * field_nums[2], LAYER_SIZES[2]), dtype=jnp.float32) * 0.05
        b0 = jnp.zeros((LAYER_SIZES[0],), jnp.float32)
        b1 = jnp.zeros((LAYER_SIZES[1],), jnp.float32)
        b2 = jnp.zeros((LAYER_SIZES[2],), jnp.float32)
        return {'x': x, 'W0': W0, 'W1': W1, 'W2': W2, 'b0': b0, 'b1': b1, 'b2': b2}
    _L0_rec_all = _L0_rec_setup()
    _L0_rec_in = {k: v for k, v in _L0_rec_all.items() if k in ('W0', 'W1', 'W2', 'b0', 'b1', 'b2')}
    del _L0_rec_all
    return {'dense_ctx': dense_ctx, 'ids': ids, 'tbl_0': tbl_0, 'tbl_1': tbl_1, 'tbl_2': tbl_2, 'tbl_3': tbl_3, 'tbl_4': tbl_4, 'tbl_5': tbl_5, 'tbl_6': tbl_6, 'tbl_7': tbl_7, 'tbl_8': tbl_8, 'tbl_9': tbl_9, 'tbl_10': tbl_10, 'tbl_11': tbl_11, 'tbl_12': tbl_12, 'tbl_13': tbl_13, 'tbl_14': tbl_14, 'tbl_15': tbl_15, 'tbl_16': tbl_16, 'tbl_17': tbl_17, 'tbl_18': tbl_18, 'tbl_19': tbl_19, 'tbl_20': tbl_20, 'tbl_21': tbl_21, 'tbl_22': tbl_22, 'tbl_23': tbl_23, 'tbl_24': tbl_24, 'tbl_25': tbl_25, 'tbl_26': tbl_26, 'tbl_27': tbl_27, 'tbl_28': tbl_28, 'tbl_29': tbl_29, 'tbl_30': tbl_30, 'tbl_31': tbl_31, 'tbl_32': tbl_32, 'tbl_33': tbl_33, 'tbl_34': tbl_34, 'tbl_35': tbl_35, 'tbl_36': tbl_36, 'tbl_37': tbl_37, 'tbl_38': tbl_38, 'W_top1': W_top1, 'b_top1': b_top1, 'W_top2': W_top2, 'b_top2': b_top2, 'W_top3': W_top3, 'L0_rec_W0': _L0_rec_in['W0'], 'L0_rec_W1': _L0_rec_in['W1'], 'L0_rec_W2': _L0_rec_in['W2'], 'L0_rec_b0': _L0_rec_in['b0'], 'L0_rec_b1': _L0_rec_in['b1'], 'L0_rec_b2': _L0_rec_in['b2']}

def reference(dense_ctx, ids, tbl_0, tbl_1, tbl_2, tbl_3, tbl_4, tbl_5, tbl_6, tbl_7, tbl_8, tbl_9, tbl_10, tbl_11, tbl_12, tbl_13, tbl_14, tbl_15, tbl_16, tbl_17, tbl_18, tbl_19, tbl_20, tbl_21, tbl_22, tbl_23, tbl_24, tbl_25, tbl_26, tbl_27, tbl_28, tbl_29, tbl_30, tbl_31, tbl_32, tbl_33, tbl_34, tbl_35, tbl_36, tbl_37, tbl_38, W_top1, b_top1, W_top2, b_top2, W_top3, L0_rec_W0, L0_rec_W1, L0_rec_W2, L0_rec_b0, L0_rec_b1, L0_rec_b2):
    import jax
    import jax.numpy as jnp

    def _L0_rec_ref(x, W0, W1, W2, b0, b1, b2):
        import jax, jax.numpy as jnp
        import numpy as np
        LAYER_SIZES = [128, 128, 128]
        F0 = 39
        D = 16
        B = 256
        Ws = [W0, W1, W2]
        bs = [b0, b1, b2]
        h = x
        outs = []
        n_layers = len(LAYER_SIZES)
        for i, S in enumerate(LAYER_SIZES):
            Fk = h.shape[1]
            Wr = Ws[i].reshape(F0, Fk, S)
            out = jax.nn.relu(jnp.einsum('bfd,bgd,fgs->bsd', x, h, Wr) + bs[i][None, :, None])
            if i != n_layers - 1:
                h, direct = (out[:, :S // 2], out[:, S // 2:])
            else:
                direct = out
            outs.append(direct)
        result = jnp.concatenate(outs, axis=1)
        return jnp.sum(result, axis=-1)
    e = jnp.stack([tbl_0[ids[:, 0]], tbl_1[ids[:, 1]], tbl_2[ids[:, 2]], tbl_3[ids[:, 3]], tbl_4[ids[:, 4]], tbl_5[ids[:, 5]], tbl_6[ids[:, 6]], tbl_7[ids[:, 7]], tbl_8[ids[:, 8]], tbl_9[ids[:, 9]], tbl_10[ids[:, 10]], tbl_11[ids[:, 11]], tbl_12[ids[:, 12]], tbl_13[ids[:, 13]], tbl_14[ids[:, 14]], tbl_15[ids[:, 15]], tbl_16[ids[:, 16]], tbl_17[ids[:, 17]], tbl_18[ids[:, 18]], tbl_19[ids[:, 19]], tbl_20[ids[:, 20]], tbl_21[ids[:, 21]], tbl_22[ids[:, 22]], tbl_23[ids[:, 23]], tbl_24[ids[:, 24]], tbl_25[ids[:, 25]], tbl_26[ids[:, 26]], tbl_27[ids[:, 27]], tbl_28[ids[:, 28]], tbl_29[ids[:, 29]], tbl_30[ids[:, 30]], tbl_31[ids[:, 31]], tbl_32[ids[:, 32]], tbl_33[ids[:, 33]], tbl_34[ids[:, 34]], tbl_35[ids[:, 35]], tbl_36[ids[:, 36]], tbl_37[ids[:, 37]], tbl_38[ids[:, 38]]], axis=1)
    z = _L0_rec_ref(e, L0_rec_W0, L0_rec_W1, L0_rec_W2, L0_rec_b0, L0_rec_b1, L0_rec_b2)
    z = z.reshape(z.shape[0], -1)
    h = jnp.concatenate([z, dense_ctx], axis=1)
    h = jnp.maximum(h @ W_top1 + b_top1, 0.0)
    h = jnp.maximum(h @ W_top2 + b_top2, 0.0)
    y = h @ W_top3
    return y

_drawn_inputs = setup_inputs


def setup_inputs(seed=0):
    import zlib

    import numpy as np

    out = dict(_drawn_inputs(seed))
    spreads = {'b_top1': (0.0, 0.8),
     'b_top2': (0.0, 0.8),
     'L0_rec_b0': (0.0, 0.338),
     'L0_rec_b1': (0.0, 0.522),
     'L0_rec_b2': (0.0, 0.311)}
    factors = {'tbl_0': 8.0,
     'tbl_1': 8.0,
     'tbl_2': 8.0,
     'tbl_3': 8.0,
     'tbl_4': 8.0,
     'tbl_5': 8.0,
     'tbl_6': 8.0,
     'tbl_7': 8.0,
     'tbl_8': 8.0,
     'tbl_9': 8.0,
     'tbl_10': 8.0,
     'tbl_11': 8.0,
     'tbl_12': 8.0,
     'tbl_13': 8.0,
     'tbl_14': 8.0,
     'tbl_15': 8.0,
     'tbl_16': 8.0,
     'tbl_17': 8.0,
     'tbl_18': 8.0,
     'tbl_19': 8.0,
     'tbl_20': 8.0,
     'tbl_21': 8.0,
     'tbl_22': 7.173,
     'tbl_23': 8.0,
     'tbl_24': 8.0,
     'tbl_25': 8.0,
     'tbl_26': 7.45,
     'tbl_27': 8.0,
     'tbl_28': 8.0,
     'tbl_29': 8.0,
     'tbl_30': 8.0,
     'tbl_31': 7.471,
     'tbl_32': 8.0,
     'tbl_33': 8.0,
     'tbl_34': 8.0,
     'tbl_35': 8.0,
     'tbl_36': 8.0,
     'tbl_37': 8.0,
     'tbl_38': 8.0,
     'L0_rec_W0': 6.995,
     'L0_rec_W1': 3.351,
     'dense_ctx': 6.696}
    for name, (base, spread) in spreads.items():
        noise = np.random.default_rng([zlib.crc32(name.encode()), seed]).standard_normal(out[name].shape)
        drawn = base * np.exp(spread * noise) if base else spread * noise
        out[name] = jnp.asarray(drawn.astype(out[name].dtype))
    for name, factor in factors.items():
        out[name] = (out[name] * factor).astype(out[name].dtype)
    return out
```

```python
from contextlib import ExitStack

import concourse.bass as bass
from concourse import mybir

F32 = mybir.dt.float32
I32 = mybir.dt.int32
ALU = mybir.AluOpType
ACT = mybir.ActivationFunctionType
AX_X = mybir.AxisListType.X

P = 128
B = 512
F = 39
D = 16
S = 128
H = S // 2
TB = 32
COLS = TB * D
NT = B // TB
FPG = P // TB
NG = -(-F // FPG)
LASTG = (F - FPG * (NG - 1)) * TB
NSHIFT = (F + 1) // 2
SPC = P // F
R0 = SPC * F
C0 = -(-NSHIFT // SPC)
C12 = -(-F * H // P)
XROWS = F + C0 * SPC - 1
UNIT = 2
U0 = -(-C0 // UNIT)
U12 = C12 // UNIT
UPT = 2 * U12 + U0
RING = 4
GROUPS = 2
CPG = C12 // GROUPS
NDENSE = 16
M1, M2 = 512, 256


def build(nc, ids, row_base, tables, w0a, w0b, w1, w2, biases, dense, wt1, bt1, wt2, bt2, wt3, out):
    x_dram = nc.dram_tensor("x_rows", (NT, XROWS, COLS), F32)

    with ExitStack() as ctx:
        def sb(name, shape, dt=F32):
            return ctx.enter_context(nc.sbuf_tensor(name, shape, dt))

        def psum(name):
            return ctx.enter_context(nc.psum_tensor(name, [P, COLS], F32))

        def sem(name):
            return ctx.enter_context(nc.semaphore(name))

        ids_sb = sb("ids_sb", [P, NT * NG], I32)
        base_sb = sb("base_sb", [P, NG], I32)
        index = [sb(f"index{s}", [P, NG], I32) for s in range(2)]
        gathered = [sb(f"gathered{s}", [P, NG, D]) for s in range(2)]
        x_rep = [sb(f"x_rep{s}", [P, C12, COLS]) for s in range(2)]
        x_shift = [sb(f"x_shift{s}", [P, C0, COLS]) for s in range(2)]
        x_stack = [sb(f"x_stack{s}", [P, COLS]) for s in range(2)]
        prod = sb("prod", [P, RING, UNIT, COLS])
        w0_sb = sb("w0_sb", [P, C0, S])
        w0b_sb = sb("w0b_sb", [P, C0, S])
        w1_sb = sb("w1_sb", [P, C12, S])
        w2_sb = sb("w2_sb", [P, C12, S])
        bias = sb("bias", [P, 3])
        bias_t1 = sb("bias_t1", [P, M1 // P])
        bias_t2 = sb("bias_t2", [P, M2 // P])
        direct0 = sb("direct0", [P, COLS])
        direct1 = sb("direct1", [P, COLS])
        direct2 = sb("direct2", [P, COLS])
        z01 = sb("z01", [P, B])
        z2 = sb("z2", [P, B])
        dense_sb = sb("dense_sb", [NDENSE, B])
        wt1_z01 = sb("wt1_z01", [P, M1])
        wt1_z2 = sb("wt1_z2", [P, M1])
        wt1_dense = sb("wt1_dense", [NDENSE, M1])
        wt2_sb = sb("wt2_sb", [P, M1 // P, M2])
        wt3_sb = sb("wt3_sb", [P, M2 // P])
        top1 = sb("top1", [P, M1 // P, B])
        top2 = sb("top2", [P, M2 // P, B])
        y_sb = sb("y_sb", [1, B])

        acc = [psum(f"acc{n}") for n in range(3)]
        x_ps = psum("x_ps")
        h_ps = [psum("h1_ps"), psum("h2_ps")]
        top_ps = [psum("top_a"), psum("top_b")]

        ids_in = sem("ids_in")
        w0_in = sem("w0_in")
        w1_in = sem("w1_in")
        w2_in = sem("w2_in")
        top_in = sem("top_in")
        bias_in = sem("bias_in")
        w0_summed = sem("w0_summed")
        index_ready = sem("index_ready")
        gather_done = [sem(f"gather_done{s}") for s in range(2)]
        rows_written = [sem(f"rows_written{s}") for s in range(2)]
        x_shift_in = [sem(f"x_shift_in{s}") for s in range(2)]
        x_stack_in = [sem(f"x_stack_in{s}") for s in range(2)]
        x_rep_in = [[sem(f"x_rep_in{s}_{g}") for g in range(GROUPS)] for s in range(2)]
        x_ps_ready = sem("x_ps_ready")
        prod_ready = sem("prod_ready")
        prod_used = sem("prod_used")
        h_ready = [sem("h1_ready"), sem("h2_ready")]
        direct_ready = [sem(f"direct_ready{n}") for n in range(3)]
        z_ready = sem("z_ready")
        top_acc = sem("top_acc")
        top_relu = sem("top_relu")
        y_ready = sem("y_ready")
        y_out = sem("y_out")

        def first_unit(t):
            return U0 + UPT * t

        def size(unit, chunks):
            return min(UNIT, chunks - UNIT * unit)

        def top_bank(m):
            return (top_ps[0], top_ps[1], acc[0], acc[1], h_ps[0], h_ps[1])[m]

        block = ctx.enter_context(nc.Block())

        @block.gpsimd
        def _(pool):
            def gather(t, s):
                nc.gpsimd.tensor_tensor(index[s][:], ids_sb[:, bass.ds(t * NG, NG)], base_sb[:],
                                        ALU.add).then_inc(index_ready, 1)
                pool.wait_ge(index_ready, t + 1)
                for j in range(NG):
                    n = P if j < NG - 1 else LASTG
                    nc.gpsimd.indirect_dma_start(
                        gathered[s][0:n, j, :], None, tables[:, :],
                        bass.IndirectOffsetOnAxis(ap=index[s][0:n, j:j + 1], axis=0),
                    ).then_inc(gather_done[s], 16)

            pool.wait_ge(ids_in, 32)
            for s in range(2):
                gather(s, s)
            for t in range(2, NT):
                pool.wait_ge(rows_written[t % 2], t // 2 * 48)
                gather(t, t % 2)

        @block.sync
        def _(sp):
            def write_rows(t, s, nth):
                sp.wait_ge(gather_done[s], nth * (16 * NG))
                full = FPG * (NG - 1)
                again = -(-(XROWS - F) // FPG)
                rows = x_dram[bass.ds(t, 1)].rearrange("a r n -> (a r) n")
                sp.dma_start(rows[0:full].rearrange("(j f) (b d) -> (f b) j d", f=FPG, d=D),
                             gathered[s][:, 0:NG - 1, :]).then_inc(rows_written[s], 16)
                sp.dma_start(rows[full:F].rearrange("f (b d) -> (f b) d", d=D),
                             gathered[s][0:LASTG, NG - 1, :]).then_inc(rows_written[s], 16)
                sp.dma_start(rows[F:F + again * FPG].rearrange("(j f) (b d) -> (f b) j d", f=FPG, d=D),
                             gathered[s][:, 0:again, :]).then_inc(rows_written[s], 16)

            def load_layer0(t, s):
                for k in range(SPC):
                    sp.dma_start(x_shift[s][k * F:(k + 1) * F],
                                 bass.AP(x_dram, (t * XROWS + k) * COLS,
                                         [[COLS, F], [SPC * COLS, C0], [1, COLS]])).then_inc(x_shift_in[s], 16)
                for k in range(SPC):
                    sp.dma_start(x_stack[s][k * F:(k + 1) * F],
                                 bass.AP(x_dram, t * (XROWS * COLS), [[COLS, F], [1, COLS]])
                                 ).then_inc(x_stack_in[s], 16)

            def load_rep(t, s):
                for g in range(GROUPS):
                    for half in range(2):
                        sp.dma_start(x_rep[s][half * H:(half + 1) * H, g * CPG:(g + 1) * CPG],
                                     bass.AP(x_dram, (t * XROWS + (2 * g * CPG + half)) * COLS,
                                             [[0, H], [2 * COLS, CPG], [1, COLS]])).then_inc(x_rep_in[s][g], 16)

            sp.dma_start(ids_sb[:], ids).then_inc(ids_in, 16)
            sp.dma_start(base_sb[:], row_base).then_inc(ids_in, 16)
            sp.dma_start(w0_sb[0:R0], w0a).then_inc(w0_in, 16)
            sp.dma_start(w0b_sb[0:R0], w0b).then_inc(w0_in, 16)
            sp.dma_start(bias[:], biases).then_inc(bias_in, 16)
            write_rows(0, 0, 1)
            sp.wait_ge(rows_written[0], 48)
            load_layer0(0, 0)
            load_rep(0, 0)
            for w, w_sb, w_in in ((w1, w1_sb, w1_in), (w2, w2_sb, w2_in)):
                sp.dma_start(w_sb[:, 0:C12 - 1], w[0:(C12 - 1) * P].rearrange("(c p) s -> p c s", p=P)).then_inc(w_in, 16)
                sp.dma_start(w_sb[0:H, C12 - 1], w[(C12 - 1) * P:F * H]).then_inc(w_in, 16)
            write_rows(1, 1, 1)
            sp.wait_ge(rows_written[1], 48)
            load_layer0(1, 1)
            write_rows(2, 0, 2)
            for dst, src in (
                (wt1_z01[0:H], wt1[H:2 * H]), (wt1_z01[H:P], wt1[0:H]), (wt1_z2[:], wt1[2 * H:2 * H + P]),
                (wt1_dense[:], wt1[2 * H + P:2 * H + P + NDENSE]), (dense_sb[:], dense),
                (wt2_sb[:], wt2.rearrange("(c p) n -> p c n", p=P)),
                (wt3_sb[:], wt3), (bias_t1[:], bt1), (bias_t2[:], bt2),
            ):
                sp.dma_start(dst, src).then_inc(top_in, 16)
            load_rep(1, 1)
            sp.wait_ge(prod_ready, U0)
            sp.wait_ge(rows_written[0], 96)
            load_layer0(2, 0)
            write_rows(3, 1, 2)

            def tile(t, s, nth, ahead0, ahead1):
                if ahead0:
                    sp.wait_ge(rows_written[1 - s], (nth + s) * 48)
                    sp.wait_ge(prod_ready, first_unit(t - 2) + U12 + U0)
                    load_layer0(t + 1, 1 - s)
                sp.wait_ge(prod_ready, first_unit(t - 1))
                load_rep(t, s)
                if ahead1:
                    write_rows(t + 2, s, nth + 1)

            for t in range(2, NT):
                tile(t, t % 2, t // 2 + 1, t + 1 < NT, t + 2 < NT)
            sp.wait_ge(y_ready, 1)
            sp.dma_start(out.rearrange("b a -> a b"), y_sb[:]).then_inc(y_out, 16)
            sp.wait_ge(y_out, 16)

        @block.vector
        def _(dve):
            def multiply(n, u, g, rows, x, h):
                if not isinstance(g, int) or g >= RING:
                    dve.wait_ge(prod_used, g - (RING - 1))
                slot = slot_of(g)
                nc.vector.tensor_tensor(prod[0:rows, slot, 0:n], x[0:rows, UNIT * u:UNIT * u + n],
                                        bass.AP(h, 0, [[COLS, rows], [0, n], [1, COLS]]),
                                        ALU.mult).then_inc(prod_ready, 1)

            slot = [0]

            def slot_of(g):
                s = slot[0]
                slot[0] = (s + 1) % RING
                return s

            def layer0(t_unit, s, nth):
                dve.wait_ge(x_shift_in[s], nth * (16 * SPC))
                for u in range(U0):
                    multiply(size(u, C0), u, t_unit + u, R0, x_shift[s], x_ps)

            def sum_dims(n, t):
                dve.wait_ge(direct_ready[n], t + 1)
                src, dst = ((direct0[H:P], z01[H:P]), (direct1[H:P], z01[0:H]), (direct2[:], z2[:]))[n]
                nc.vector.tensor_reduce(dst[:, bass.ds(t * TB, TB)], src.rearrange("p (b d) -> p b d", d=D),
                                        AX_X, ALU.add).then_inc(z_ready, 1)

            def tile(t, s, nth, first, last):
                g = first_unit(t)
                for u in range(U12):
                    if u == 0:
                        dve.wait_ge(h_ready[0], (t + 1) * 2)
                    if UNIT * u % CPG == 0:
                        dve.wait_ge(x_rep_in[s][UNIT * u // CPG], nth * 32)
                    multiply(UNIT, u, g + u, P, x_rep[s], h_ps[0])
                    if u == U12 // 2:
                        sum_dims(0, t)
                        if not first:
                            sum_dims(2, t - 1)
                g = g + U12
                if not last:
                    dve.wait_ge(x_ps_ready, t + 2)
                    layer0(g, 1 - s, nth + s)
                    g = g + U0
                dve.wait_ge(h_ready[1], (t + 1) * 2)
                for u in range(U12):
                    multiply(UNIT, u, g + u, P, x_rep[s], h_ps[1])
                    if u == U12 // 2:
                        sum_dims(1, t)

            dve.wait_ge(w0_in, 32)
            nc.vector.tensor_tensor(w0_sb[0:R0], w0_sb[0:R0], w0b_sb[0:R0], ALU.add).then_inc(w0_summed, 1)
            dve.wait_ge(x_ps_ready, 1)
            layer0(0, 0, 1)
            for s in range(2):
                tile(s, s, 1, s == 0, False)
            with dve.Fori(1, NT // 2 - 1) as i:
                for s in range(2):
                    tile(i * 2 + s, s, i + 1, False, False)
            for s in range(2):
                tile(NT - 2 + s, s, NT // 2, False, s == 1)
            sum_dims(2, NT - 1)

        @block.scalar
        def _(act):
            def stack(t, s, nth):
                act.wait_ge(x_stack_in[s], nth * (16 * SPC))
                nc.scalar.copy(x_ps[0:R0], x_stack[s][0:R0]).then_inc(x_ps_ready, 1)

            def outputs(n, units):
                act.wait_ge(prod_used, units)
                if n < 2:
                    for half in range(2):
                        nc.scalar.activation(h_ps[n][half * H:(half + 1) * H], acc[n][0:H], ACT.Relu,
                                             bias=bias[0:H, n:n + 1]).then_inc(h_ready[n], 1)
                lo = H if n < 2 else 0
                dst = (direct0, direct1, direct2)[n]
                nc.scalar.activation(dst[lo:P], acc[n][lo:P], ACT.Relu,
                                     bias=bias[lo:P, n:n + 1]).then_inc(direct_ready[n], 1)

            def tile(t, s, nth, last):
                if not last:
                    stack(t + 1, 1 - s, nth + s)
                g = first_unit(t) + U12
                outputs(1, g)
                if not last:
                    g = g + U0
                    outputs(0, g)
                outputs(2, g + U12)

            stack(0, 0, 1)
            act.wait_ge(bias_in, 16)
            outputs(0, U0)
            with act.Fori(0, NT // 2 - 1) as i:
                for s in range(2):
                    tile(i * 2 + s, s, i + 1, False)
            for s in range(2):
                tile(NT - 2 + s, s, NT // 2, s == 1)
            act.wait_ge(top_in, 16 * 9)
            done = 0
            for m in range(M1 // P):
                done += 1
                act.wait_ge(top_acc, done)
                nc.scalar.activation(top1[:, m], top_bank(m)[:], ACT.Relu,
                                     bias=bias_t1[:, m:m + 1]).then_inc(top_relu, 1)
            for m in range(M2 // P):
                done += 1
                act.wait_ge(top_acc, done)
                nc.scalar.activation(top2[:, m], top_bank(M1 // P + m)[:], ACT.Relu,
                                     bias=bias_t2[:, m:m + 1]).then_inc(top_relu, 1)
            act.wait_ge(top_acc, done + 1)
            nc.scalar.copy(y_sb[:], top_bank(0)[0:1]).then_inc(y_ready, 1)

        @block.tensor
        def _(pe):
            slot = [0]

            def contract(n, chunks, w, g0):
                for u in range(-(-chunks // UNIT)):
                    pe.wait_ge(prod_ready, g0 + (u + 1))
                    for k in range(size(u, chunks)):
                        c = UNIT * u + k
                        if n == 0:
                            rows = min(R0, (NSHIFT - SPC * c) * F)
                        else:
                            rows = min(P, F * H - P * c)
                        mm = nc.tensor.matmul(acc[n][:], w[0:rows, c], prod[0:rows, slot[0], k],
                                              start=(c == 0), stop=(c == chunks - 1))
                    mm.then_inc(prod_used, 1)
                    slot[0] = (slot[0] + 1) % RING

            def tile(t, last):
                g = first_unit(t)
                contract(1, C12, w1_sb, g)
                g = g + U12
                if not last:
                    pe.wait_ge(direct_ready[0], t + 1)
                    contract(0, C0, w0_sb, g)
                    g = g + U0
                contract(2, C12, w2_sb, g)

            pe.wait_ge(w0_summed, 1)
            contract(0, C0, w0_sb, 0)
            pe.wait_ge(w1_in, 32)
            pe.wait_ge(w2_in, 32)
            with pe.Fori(0, NT // 2 - 1) as i:
                for s in range(2):
                    tile(i * 2 + s, False)
            for s in range(2):
                tile(NT - 2 + s, s == 1)
            pe.wait_ge(top_in, 16 * 9)
            pe.wait_ge(z_ready, 3 * NT)
            for m in range(M1 // P):
                cols = slice(m * P, (m + 1) * P)
                nc.tensor.matmul(top_bank(m)[:], wt1_dense[:, cols], dense_sb[:], start=True, stop=False)
                nc.tensor.matmul(top_bank(m)[:], wt1_z01[:, cols], z01[:], start=False, stop=False)
                nc.tensor.matmul(top_bank(m)[:], wt1_z2[:, cols], z2[:], start=False, stop=True).then_inc(top_acc, 1)
            for m in range(M2 // P):
                for c in range(M1 // P):
                    if m == 0:
                        pe.wait_ge(top_relu, c + 1)
                    mm = nc.tensor.matmul(top_bank(M1 // P + m)[:], wt2_sb[:, c, m * P:(m + 1) * P], top1[:, c],
                                          start=(c == 0), stop=(c == M1 // P - 1))
                mm.then_inc(top_acc, 1)
            for c in range(M2 // P):
                pe.wait_ge(top_relu, M1 // P + c + 1)
                mm = nc.tensor.matmul(top_bank(0)[0:1], wt3_sb[:, c:c + 1], top2[:, c],
                                      start=(c == 0), stop=(c == M2 // P - 1))
            mm.then_inc(top_acc, 1)


def lay_out(np, inputs):
    tables = [np.asarray(inputs[f"tbl_{f}"]) for f in range(F)]
    ids = np.asarray(inputs["ids"])
    padded = np.zeros((NG * FPG, B), ids.dtype)
    padded[:F] = ids.T
    ids_laid = np.ascontiguousarray(padded.reshape(NG, FPG, NT, TB).transpose(1, 3, 2, 0).reshape(P, NT * NG))
    starts = np.zeros(NG * FPG, ids.dtype)
    starts[1:F] = np.cumsum([t.shape[0] for t in tables])[:F - 1]
    row_base = np.ascontiguousarray(np.repeat(starts.reshape(NG, FPG).T, TB, axis=0))
    w0 = np.asarray(inputs["L0_rec_W0"]).reshape(F, F, S)
    f = np.arange(F)
    w0a = np.zeros((C0 * SPC, F, S), w0.dtype)
    w0b = np.zeros((C0 * SPC, F, S), w0.dtype)
    for k in range(NSHIFT):
        w0a[k] = w0[f, (f + k) % F]
        if k:
            w0b[k] = w0[(f + k) % F, f]

    def chunks(w):
        return np.ascontiguousarray(w.reshape(C0, R0, S).transpose(1, 0, 2))

    def by_partition(v):
        return np.ascontiguousarray(np.asarray(v).reshape(-1, P).T)

    return {
        "ids": ids_laid, "row_base": row_base, "tables": np.concatenate(tables, axis=0),
        "w0a": chunks(w0a), "w0b": chunks(w0b),
        "w1": np.asarray(inputs["L0_rec_W1"]), "w2": np.asarray(inputs["L0_rec_W2"]),
        "biases": by_partition(np.stack([np.asarray(inputs[f"L0_rec_b{n}"]) for n in range(3)])),
        "dense": np.ascontiguousarray(np.asarray(inputs["dense_ctx"]).T),
        "wt1": np.asarray(inputs["W_top1"]), "bt1": by_partition(inputs["b_top1"]),
        "wt2": np.asarray(inputs["W_top2"]), "bt2": by_partition(inputs["b_top2"]),
        "wt3": by_partition(inputs["W_top3"]),
    }


def kernel(**inputs):
    import numpy as np
    import concourse.bacc as bacc
    from concourse.bass_utils import run_bass_kernel_spmd

    nc = bacc.Bacc("TRN2", target_bir_lowering=False, num_devices=1)
    arrays, args = {}, []
    for name, a in lay_out(np, inputs).items():
        arrays[f"in_{name}"] = a
        args.append(nc.dram_tensor(f"in_{name}", a.shape, mybir.dt.from_np(a.dtype), kind="ExternalInput").ap())
    out = nc.dram_tensor("out_y", (B, 1), F32, kind="ExternalOutput").ap()
    build(nc, *args, out)
    r = run_bass_kernel_spmd(nc, [arrays], core_ids=[0])
    return r.results[0]["out_y"]
```

```python
from contextlib import ExitStack

import concourse.bass as bass
from concourse import mybir

F32 = mybir.dt.float32
F32R = mybir.dt.float32r
I32 = mybir.dt.int32
ALU = mybir.AluOpType
ACT = mybir.ActivationFunctionType
AX_X = mybir.AxisListType.X

P = 128
B = 512
F = 39
D = 16
S = 128
H = S // 2
TB = 32
COLS = TB * D
NT = B // TB
FPG = P // TB
NG = -(-F // FPG)
LASTG = (F - FPG * (NG - 1)) * TB
NSHIFT = (F + 1) // 2
SPC = P // F
R0 = SPC * F
C0 = -(-NSHIFT // SPC)
C12 = -(-F * H // P)
XROWS = F + C0 * SPC - 1
UNIT = 2
WHOLE, POOL, VECTOR = "whole", "pool", "vector"
KINDS = [
    [WHOLE, POOL, WHOLE, WHOLE],
    [POOL, WHOLE, POOL, VECTOR, POOL, WHOLE, POOL, VECTOR, POOL, WHOLE],
    [WHOLE, POOL, VECTOR, POOL, WHOLE, POOL, VECTOR, POOL, WHOLE, WHOLE],
]
ORDER = [
    [0, 2, 3, 1],
    [1, 0, 3, 2, 5, 4, 7, 6, 9, 8],
    [0, 2, 1, 4, 3, 6, 5, 8, 7, 9],
]
CHUNKS = [C0, C12, C12]
PROD_RING = 5
PART_RING = 4
GROUPS = [(0, 10, 2), (10, 14, 1), (14, 20, 1)]
GATHER_AHEAD = 3
NDENSE = 16
M1, M2 = 512, 256


def unit_chunks(layer, u):
    return range(UNIT * u, min(UNIT * (u + 1), CHUNKS[layer]))


def chunk_rows(layer, c):
    return min(R0, (NSHIFT - SPC * c) * F) if layer == 0 else min(P, F * H - P * c)


def weight_places():
    places = []
    for layer in range(3):
        at, whole, split = {}, 0, 0
        for u, kind in enumerate(KINDS[layer]):
            for c in unit_chunks(layer, u):
                if kind == WHOLE:
                    at[c], whole = whole, whole + 1
                else:
                    at[c], split = split, split + 1
        places.append((at, whole, split))
    return places


PLACES = weight_places()
W_WHOLE = [sum(PLACES[n][1] for n in range(m)) for m in range(4)]
W_SPLIT = [sum(PLACES[n][2] for n in range(m)) for m in range(4)]


class Counts:

    def __init__(self):
        self.nth = {}
        self.of_kind = {}
        self.split = {}
        self.used = {}
        self.prod_before = {}
        self.part_before = {}
        self.prod_slot, self.part_slot = {}, {}
        phases = [(0, 0)]
        for t in range(NT):
            phases += [(1, t)] + ([(0, t + 1)] if t + 1 < NT else []) + [(2, t)]
        kinds = {WHOLE: 0, POOL: 0, VECTOR: 0}
        rings, parts = [], []
        used = [0, 0]
        for layer, t in phases:
            for u, kind in enumerate(KINDS[layer]):
                key = (layer, t, u)
                self.nth[key] = len(self.nth)
                self.of_kind[key] = kinds[kind]
                kinds[kind] += 1
                if kind != VECTOR:
                    self.prod_before[key] = rings[-PROD_RING] if len(rings) >= PROD_RING else None
                    self.prod_slot[key] = len(rings) % PROD_RING
                    rings.append(key)
                if kind != WHOLE:
                    self.part_before[key] = parts[-PART_RING] if len(parts) >= PART_RING else None
                    self.part_slot[key] = self.split[key] = len(parts) % PART_RING
                    self.split[key] = len(parts)
                    parts.append(key)
            for u in ORDER[layer]:
                n = KINDS[layer][u] != WHOLE
                self.used[(layer, t, u)] = used[n]
                used[n] += 1


def build(nc, ids, row_base, tables, w0a, w0b, w12, w_splits, biases, dense, wt1, bt1, wt2, bt2, wt3, out):
    x_dram = nc.dram_tensor("x_rows", (NT, XROWS, COLS), F32)
    counts = Counts()

    with ExitStack() as ctx:
        def sb(name, shape, dt=F32):
            return ctx.enter_context(nc.sbuf_tensor(name, shape, dt))

        def psum(name, banks=1):
            return ctx.enter_context(nc.psum_tensor(name, [P, COLS] if banks == 1 else [P, banks, COLS], F32))

        def sem(name):
            return ctx.enter_context(nc.semaphore(name))

        ids_sb = sb("ids_sb", [P, NT * NG], I32)
        base_sb = sb("base_sb", [P, NG], I32)
        index = [sb(f"index{s}", [P, NG], I32) for s in range(2)]
        gathered = [sb(f"gathered{s}", [P, NG, D]) for s in range(2)]
        x_rep = [[sb(f"x_rep{g}_{s}", [P, hi - lo, COLS]) for s in range(n)] for g, (lo, hi, n) in enumerate(GROUPS)]
        x_shift = sb("x_shift", [P, C0, COLS])
        x_stack = sb("x_stack", [P, COLS])
        prod = sb("prod", [P, PROD_RING, UNIT, COLS])
        high = sb("high", [P, PART_RING, UNIT, COLS], F32R)
        low = sb("low", [P, PART_RING, UNIT, COLS], F32R)
        w0a_sb = sb("w0a_sb", [P, C0, S])
        w0b_sb = x_rep[0][1][:, 8:10].rearrange("p c n -> p (c n)")[:, 0:C0 * S].rearrange("p (c s) -> p c s", s=S)
        w_whole = sb("w_whole", [P, W_WHOLE[3] - W_WHOLE[1], S])
        w_high = sb("w_high", [P, W_SPLIT[3], S], F32R)
        w_low = sb("w_low", [P, W_SPLIT[3], S], F32R)
        NSPLIT = W_SPLIT[3] - W_SPLIT[1]
        w_raw = x_rep[0][1][:, 0:8].rearrange("p c n -> p (c n)")[:, 0:NSPLIT * S].rearrange("p (c s) -> p c s", s=S)
        bias = sb("bias", [P, 3])
        bias_t1 = sb("bias_t1", [P, M1 // P])
        bias_t2 = sb("bias_t2", [P, M2 // P])
        direct01 = sb("direct01", [P, COLS])
        direct2 = sb("direct2", [P, COLS])
        z01 = sb("z01", [P, B])
        z2 = sb("z2", [P, B])
        dense_sb = sb("dense_sb", [NDENSE, B])
        wt1_z = sb("wt1_z", [P, 2, M1])
        wt1_dense = sb("wt1_dense", [NDENSE, M1])
        wt2_sb = sb("wt2_sb", [P, M1 // P, M2])
        wt3_sb = sb("wt3_sb", [P, M2 // P])
        top1 = x_rep[0][0][:, 0:M1 // P]
        top2 = x_rep[0][0][:, M1 // P:(M1 + M2) // P]
        y_sb = sb("y_sb", [1, B])

        acc = [psum(f"acc{n}") for n in range(3)]
        x_ps = psum("x_ps")
        h_ps = [psum("h1_ps"), psum("h2_ps")]
        prod_ps = psum("prod_ps", UNIT)

        ids_in = sem("ids_in")
        w0_in = sem("w0_in")
        w_in = sem("w_in")
        w_raw_in = sem("w_raw_in")
        top_in = sem("top_in")
        bias_in = sem("bias_in")
        w0_summed = sem("w0_summed")
        w_high_ready = sem("w_high_ready")
        w_split = sem("w_split")
        index_ready = sem("index_ready")
        gather_done = [sem(f"gather_done{s}") for s in range(2)]
        rows_written = [sem(f"rows_written{s}") for s in range(2)]
        x_shift_in = sem("x_shift_in")
        x_stack_in = sem("x_stack_in")
        x_rep_in = [[sem(f"x_rep_in{g}_{s}") for s in range(n)] for g, (_, _, n) in enumerate(GROUPS)]
        x_ps_ready = sem("x_ps_ready")
        prod_ready = sem("prod_ready")
        high_ready = sem("high_ready")
        pool_low = sem("pool_low")
        vector_low = sem("vector_low")
        whole_used = sem("whole_used")
        split_used = sem("split_used")
        h_ready = [sem("h1_ready"), sem("h2_ready")]
        direct_ready = [sem(f"direct_ready{n}") for n in range(3)]
        z01_ready = sem("z01_ready")
        z2_ready = sem("z2_ready")
        top_acc = sem("top_acc")
        top_relu = sem("top_relu")
        y_ready = sem("y_ready")
        y_out = sem("y_out")

        def at(f, tile):
            t, i = tile
            return f(t) if i is None else i * (f(t + 2) - f(t)) + f(t)

        def multiplied(layer, tile, u=-1):
            u = u % len(KINDS[layer])
            return at(lambda t: counts.nth[layer, t, u] + 1, tile)

        def contracted(layer, tile, u=None):
            u = ORDER[layer][-1] if u is None else u
            kind = KINDS[layer][u]
            return (whole_used if kind == WHOLE else split_used), at(lambda t: counts.used[layer, t, u] + 1, tile)

        def parts_free(eng, layer, tile, u):
            before = counts.part_before[layer, tile[0], u]
            if before:
                eng.wait_ge(*contracted(before[0], (before[1], tile[1]), before[2]))

        def run_tiles(eng, tile, peeled=2):
            for t in range(2):
                tile((t, None))
            with eng.Fori(0, (NT - 2 - peeled) // 2) as i:
                for s in range(2):
                    tile((2 + s, i))
            for t in range(NT - peeled, NT):
                tile((t, None))

        def ahead(tile, n=1):
            return tile[0] + n, tile[1]

        w0_split = [(PLACES[0][0][c], c) for u, kind in enumerate(KINDS[0]) if kind != WHOLE for c in unit_chunks(0, u)]

        top_banks = [acc[0][:], acc[1][:], acc[2][:], x_ps[:], h_ps[0][:], h_ps[1][:], prod_ps[:, 0]]

        block = ctx.enter_context(nc.Block())

        @block.gpsimd
        def _(pool):
            def make_index(t, s):
                nc.gpsimd.tensor_tensor(index[s][:], ids_sb[:, bass.ds(t * NG, NG)], base_sb[:],
                                        ALU.add).then_inc(index_ready, 1)

            def gather(s, js):
                for j in js:
                    n = P if j < NG - 1 else LASTG
                    nc.gpsimd.indirect_dma_start(
                        gathered[s][0:n, j, :], None, tables[:, :],
                        bass.IndirectOffsetOnAxis(ap=index[s][0:n, j:j + 1], axis=0),
                    ).then_inc(gather_done[s], 16)

            def low_part(layer, tile, u):
                pool.wait_ge(high_ready, at(lambda t: counts.split[layer, t, u] + 1, tile))
                key = (layer, tile[0], u)
                n, rows = len(unit_chunks(layer, u)), R0 if layer == 0 else P
                ring, part = counts.prod_slot[key], counts.part_slot[key]
                nc.gpsimd.tensor_tensor(low[0:rows, part, 0:n], prod[0:rows, ring, 0:n],
                                        high[0:rows, part, 0:n].bitcast(F32), ALU.subtract).then_inc(pool_low, 1)

            def tile(tl):
                t, i = tl
                s = (t + 1) % 2
                units = [(n, ahead(tl) if n == 0 else tl, u) for n in (1, 0, 2)
                         for u, kind in enumerate(KINDS[n]) if kind == POOL and (n or t + 1 < NT)]
                more = t + GATHER_AHEAD < NT
                if more:
                    pool.wait_ge(rows_written[s], at(lambda t: (t + 1) // 2 * 48 + 48, tl))
                    ahead_t = t + GATHER_AHEAD
                    make_index(ahead_t if i is None else i * 2 + ahead_t, s)
                    pool.wait_ge(index_ready, at(lambda t: t + GATHER_AHEAD + 1, tl))
                for k, (layer, tile_, u) in enumerate(units):
                    low_part(layer, tile_, u)
                    if more:
                        gather(s, range(NG * k // len(units), NG * (k + 1) // len(units)))

            pool.wait_ge(ids_in, 32)
            for t in range(GATHER_AHEAD):
                if t >= 2:
                    pool.wait_ge(rows_written[t % 2], 48)
                make_index(t, t % 2)
                pool.wait_ge(index_ready, t + 1)
                gather(t % 2, range(NG))
            for u, kind in enumerate(KINDS[0]):
                if kind == POOL:
                    low_part(0, (0, None), u)
            run_tiles(pool, tile, peeled=GATHER_AHEAD + 1)

        @block.sync
        def _(sp):
            def write_rows(t):
                s = t % 2
                sp.wait_ge(gather_done[s], (t // 2 + 1) * (16 * NG))
                full = FPG * (NG - 1)
                again = -(-(XROWS - F) // FPG)
                rows = x_dram[t]
                sp.dma_start(rows[0:full].rearrange("(j f) (b d) -> (f b) j d", f=FPG, d=D),
                             gathered[s][:, 0:NG - 1, :]).then_inc(rows_written[s], 16)
                sp.dma_start(rows[full:F].rearrange("f (b d) -> (f b) d", d=D),
                             gathered[s][0:LASTG, NG - 1, :]).then_inc(rows_written[s], 16)
                sp.dma_start(rows[F:F + again * FPG].rearrange("(j f) (b d) -> (f b) j d", f=FPG, d=D),
                             gathered[s][:, 0:again, :]).then_inc(rows_written[s], 16)

            def rows_are_written(t):
                sp.wait_ge(rows_written[t % 2], (t // 2 + 1) * 48)

            def load_layer0(t):
                if t:
                    sp.wait_ge(prod_ready, multiplied(0, (t - 1, None)))
                for k in range(SPC):
                    sp.dma_start(x_stack[k * F:(k + 1) * F],
                                 bass.AP(x_dram, t * (XROWS * COLS), [[COLS, F], [1, COLS]])
                                 ).then_inc(x_stack_in, 16)
                for k in range(SPC):
                    sp.dma_start(x_shift[k * F:(k + 1) * F],
                                 bass.AP(x_dram, (t * XROWS + k) * COLS,
                                         [[COLS, F], [SPC * COLS, C0], [1, COLS]])).then_inc(x_shift_in, 16)

            def load_rep(t, g):
                lo, hi, n = GROUPS[g]
                if t == 1 and n == 2:
                    sp.wait_ge(w_split, W_SPLIT[1] + 1)
                elif t >= n:
                    sp.wait_ge(prod_ready, multiplied(2, (t - n, None), (hi - 1) // UNIT))
                for half in range(2):
                    sp.dma_start(x_rep[g][t % n][half * H:(half + 1) * H],
                                 bass.AP(x_dram, (t * XROWS + (2 * lo + half)) * COLS,
                                         [[0, H], [2 * COLS, hi - lo], [1, COLS]])).then_inc(x_rep_in[g][t % n], 16)

            sp.dma_start(ids_sb[:], ids).then_inc(ids_in, 16)
            sp.dma_start(base_sb[:], row_base).then_inc(ids_in, 16)
            sp.dma_start(w0a_sb[0:R0], w0a).then_inc(w0_in, 16)
            sp.dma_start(w0b_sb[0:R0], w0b).then_inc(w0_in, 16)
            sp.dma_start(bias[:], biases).then_inc(bias_in, 16)
            sp.dma_start(w_whole[:], w12).then_inc(w_in, 16)
            sp.dma_start(w_raw, w_splits).then_inc(w_raw_in, 16)
            write_rows(0)
            rows_are_written(0)
            load_layer0(0)
            for g in range(len(GROUPS)):
                load_rep(0, g)
            write_rows(1)
            for dst, src in (
                (wt1_z[:], wt1[0:2 * P].rearrange("(c p) n -> p c n", p=P)),
                (wt1_dense[:], wt1[2 * P:2 * P + NDENSE]), (dense_sb[:], dense),
                (wt2_sb[:], wt2.rearrange("(c p) n -> p c n", p=P)),
                (wt3_sb[:], wt3), (bias_t1[:], bt1), (bias_t2[:], bt2),
            ):
                sp.dma_start(dst, src).then_inc(top_in, 16)
            for t in range(1, NT):
                rows_are_written(t)
                load_layer0(t)
                load_rep(t, 0)
                if t + 1 < NT:
                    write_rows(t + 1)
                for g in range(1, len(GROUPS)):
                    load_rep(t, g)
            sp.wait_ge(y_ready, 1)
            sp.dma_start(out.rearrange("b a -> a b"), y_sb[:]).then_inc(y_out, 16)
            sp.wait_ge(y_out, 16)

        @block.vector
        def _(dve):
            def multiply(layer, tile, u):
                key = (layer, tile[0], u)
                n, rows = len(unit_chunks(layer, u)), R0 if layer == 0 else P
                c = UNIT * u
                if layer == 0:
                    x, h = x_shift[0:rows, c:c + n], x_ps
                else:
                    g = next(k for k, (lo, hi, _) in enumerate(GROUPS) if lo <= c < hi)
                    lo, _, buffers = GROUPS[g]
                    if c == lo:
                        s = tile[0] % buffers
                        dve.wait_ge(x_rep_in[g][s], at(lambda t: (t // buffers + 1) * 32, tile))
                    x, h = x_rep[g][tile[0] % buffers][:, c - lo:c - lo + n], h_ps[layer - 1]
                if KINDS[layer][u] == VECTOR:
                    if counts.of_kind[key]:
                        dve.wait_ge(vector_low, at(lambda t: counts.of_kind[layer, t, u], tile))
                    to = prod_ps[0:rows, 0:n]
                else:
                    before = counts.prod_before[key]
                    if before:
                        b, of = (before[1], tile[1]), KINDS[before[0]][before[2]]
                        if of == WHOLE:
                            dve.wait_ge(*contracted(before[0], b, before[2]))
                        else:
                            dve.wait_ge(pool_low, at(lambda t: counts.of_kind[before[0], t, before[2]] + 1, b))
                    to = prod[0:rows, counts.prod_slot[key], 0:n]
                nc.vector.tensor_tensor(to, x, bass.AP(h, 0, [[COLS, rows], [0, n], [1, COLS]]),
                                        ALU.mult).then_inc(prod_ready, 1)

            def low_part(layer, tile, u):
                dve.wait_ge(high_ready, at(lambda t: counts.split[layer, t, u] + 1, tile))
                n, rows = len(unit_chunks(layer, u)), R0 if layer == 0 else P
                part = counts.part_slot[layer, tile[0], u]
                nc.vector.tensor_tensor(low[0:rows, part, 0:n], prod_ps[0:rows, 0:n],
                                        high[0:rows, part, 0:n].bitcast(F32), ALU.subtract).then_inc(vector_low, 1)

            def layer(n, tile, extra=None):
                waiting = None
                for u, kind in enumerate(KINDS[n]):
                    multiply(n, tile, u)
                    if waiting is not None:
                        low_part(n, tile, waiting)
                    waiting = u if kind == VECTOR else None
                    if extra and u == extra[0]:
                        extra[1]()

            def sum_dims(z, z_in, direct, count, done, tile):
                dve.wait_ge(z_in, at(count, tile))
                t, i = tile
                cols = bass.ds(t * TB if i is None else i * (2 * TB) + t * TB, TB)
                nc.vector.tensor_reduce(z[:, cols], direct[:].rearrange("p (b d) -> p b d", d=D),
                                        AX_X, ALU.add).then_inc(done, 1)

            def sum01(tile):
                sum_dims(z01, direct_ready[1], direct01, lambda t: t + 1, z01_ready, tile)

            def sum2(tile):
                sum_dims(z2, direct_ready[2], direct2, lambda t: t + 1, z2_ready, tile)

            def tile(tl):
                dve.wait_ge(h_ready[0], at(lambda t: 2 * t + 2, tl))
                layer(1, tl, (5, lambda: sum2(ahead(tl, -1))) if tl[0] else None)
                if tl[0] + 1 < NT:
                    nxt = ahead(tl)
                    dve.wait_ge(x_ps_ready, at(lambda t: t + 1, nxt))
                    dve.wait_ge(x_shift_in, at(lambda t: (t + 1) * (16 * SPC), nxt))
                    layer(0, nxt)
                dve.wait_ge(h_ready[1], at(lambda t: 2 * t + 2, tl))
                layer(2, tl, (2, lambda: sum01(tl)))

            dve.wait_ge(w0_in, 32)
            nc.vector.tensor_tensor(w0a_sb[0:R0], w0a_sb[0:R0], w0b_sb[0:R0], ALU.add).then_inc(w0_summed, 1)
            k = W_SPLIT[1]
            dve.wait_ge(w_high_ready, k + 1)
            for at_, c in w0_split:
                nc.vector.tensor_tensor(w_low[0:R0, at_], w0a_sb[0:R0, c], w_high[0:R0, at_].bitcast(F32),
                                        ALU.subtract).then_inc(w_split, 1)
            nc.vector.tensor_tensor(w_low[:, k:], w_raw, w_high[:, k:].bitcast(F32),
                                    ALU.subtract).then_inc(w_split, 1)
            dve.wait_ge(x_ps_ready, 1)
            dve.wait_ge(x_shift_in, 16 * SPC)
            layer(0, (0, None))
            run_tiles(dve, tile)
            sum2((NT - 1, None))

        @block.scalar
        def _(act):
            def stack(tile):
                act.wait_ge(x_stack_in, at(lambda t: (t + 1) * (16 * SPC), tile))
                nc.scalar.copy(x_ps[0:R0], x_stack[0:R0]).then_inc(x_ps_ready, 1)

            def high_part(layer, tile, u):
                kind, key = KINDS[layer][u], (layer, tile[0], u)
                if kind == WHOLE:
                    return
                parts_free(act, layer, tile, u)
                act.wait_ge(prod_ready, multiplied(layer, tile, u))
                n, rows = len(unit_chunks(layer, u)), R0 if layer == 0 else P
                src = prod_ps[0:rows, 0:n] if kind == VECTOR else prod[0:rows, counts.prod_slot[key], 0:n]
                nc.scalar.copy(high[0:rows, counts.part_slot[key], 0:n], src).then_inc(high_ready, 1)

            def layer(n, tile, extra):
                for u in range(len(KINDS[n])):
                    high_part(n, tile, u)
                    if u in extra:
                        extra[u]()

            def outputs(n, tile):
                act.wait_ge(*contracted(n, tile))
                if n == 2:
                    nc.scalar.activation(direct2[:], acc[2][:], ACT.Relu, bias=bias[:, 2:3]).then_inc(direct_ready[2], 1)
                    return
                for half in range(2):
                    nc.scalar.activation(h_ps[n][half * H:(half + 1) * H], acc[n][0:H], ACT.Relu,
                                         bias=bias[0:H, n:n + 1]).then_inc(h_ready[n], 1)
                if n == 0 and tile[0]:
                    act.wait_ge(z01_ready, at(lambda t: t, tile))
                nc.scalar.activation(direct01[n * H:(n + 1) * H], acc[n][H:P], ACT.Relu,
                                     bias=bias[H:P, n:n + 1]).then_inc(direct_ready[n], 1)

            def tile(tl):
                t = tl[0]
                more = t + 1 < NT
                extra = {}
                if t:
                    extra[4] = lambda: outputs(2, ahead(tl, -1))
                if more:
                    extra[7] = lambda: stack(ahead(tl))
                layer(1, tl, extra)
                if more:
                    layer(0, ahead(tl), {})
                outputs(1, tl)
                layer(2, tl, {7: lambda: outputs(0, ahead(tl))} if more else {})

            act.wait_ge(w0_summed, 1)
            k = W_SPLIT[1]
            for at_, c in w0_split:
                nc.scalar.copy(w_high[0:R0, at_], w0a_sb[0:R0, c]).then_inc(w_high_ready, 1)
            act.wait_ge(w_raw_in, 16)
            nc.scalar.copy(w_high[:, k:], w_raw).then_inc(w_high_ready, 1)
            stack((0, None))
            layer(0, (0, None), {})
            act.wait_ge(bias_in, 16)
            outputs(0, (0, None))
            run_tiles(act, tile)
            outputs(2, (NT - 1, None))
            act.wait_ge(top_in, 16 * 7)
            done = 0
            for m in range(M1 // P):
                done += 1
                act.wait_ge(top_acc, done)
                nc.scalar.activation(top1[:, m], top_banks[m], ACT.Relu,
                                     bias=bias_t1[:, m:m + 1]).then_inc(top_relu, 1)
            for m in range(M2 // P):
                done += 1
                act.wait_ge(top_acc, done)
                nc.scalar.activation(top2[:, m], top_banks[M1 // P + m], ACT.Relu,
                                     bias=bias_t2[:, m:m + 1]).then_inc(top_relu, 1)
            act.wait_ge(top_acc, done + 1)
            nc.scalar.copy(y_sb[:], top_banks[6][0:1]).then_inc(y_ready, 1)

        @block.tensor
        def _(pe):
            def contract(layer, tile):
                place, _, _ = PLACES[layer]
                first = True
                for u in ORDER[layer]:
                    kind, key = KINDS[layer][u], (layer, tile[0], u)
                    if kind == WHOLE:
                        pe.wait_ge(prod_ready, multiplied(layer, tile, u))
                    else:
                        pe.wait_ge(pool_low if kind == POOL else vector_low,
                                   at(lambda t: counts.of_kind[layer, t, u] + 1, tile))
                    for k, c in enumerate(unit_chunks(layer, u)):
                        rows = chunk_rows(layer, c)
                        last = u == ORDER[layer][-1] and c == unit_chunks(layer, u)[-1]
                        if kind == WHOLE:
                            w = w0a_sb[0:rows, c] if layer == 0 else w_whole[0:rows, W_WHOLE[layer] - W_WHOLE[1] + place[c]]
                            pairs = [(w, prod[0:rows, counts.prod_slot[key], k])]
                        else:
                            n, part = W_SPLIT[layer] + place[c], counts.part_slot[key]
                            hi, lo = w_high[0:rows, n], w_low[0:rows, n]
                            pairs = [(hi, low[0:rows, part, k]), (hi, high[0:rows, part, k]), (lo, high[0:rows, part, k])]
                        for m, (w, p) in enumerate(pairs):
                            mm = nc.tensor.matmul(acc[layer][:], w, p, start=first,
                                                  stop=last and m == len(pairs) - 1)
                            first = False
                    mm.then_inc(whole_used if kind == WHOLE else split_used, 1)

            def tile(tl):
                contract(1, tl)
                if tl[0] + 1 < NT:
                    pe.wait_ge(direct_ready[0], at(lambda t: t + 1, tl))
                    contract(0, ahead(tl))
                contract(2, tl)

            pe.wait_ge(w0_summed, 1)
            pe.wait_ge(w_split, W_SPLIT[1] + 1)
            contract(0, (0, None))
            pe.wait_ge(w_in, 16)
            run_tiles(pe, tile)
            pe.wait_ge(top_in, 16 * 7)
            pe.wait_ge(z01_ready, NT)
            pe.wait_ge(z2_ready, NT)
            for m in range(M1 // P):
                cols = slice(m * P, (m + 1) * P)
                nc.tensor.matmul(top_banks[m], wt1_dense[:, cols], dense_sb[:], start=True, stop=False)
                nc.tensor.matmul(top_banks[m], wt1_z[:, 0, cols], z01[:], start=False, stop=False)
                nc.tensor.matmul(top_banks[m], wt1_z[:, 1, cols], z2[:], start=False, stop=True).then_inc(top_acc, 1)
            for m in range(M2 // P):
                for c in range(M1 // P):
                    if m == 0:
                        pe.wait_ge(top_relu, c + 1)
                    mm = nc.tensor.matmul(top_banks[M1 // P + m], wt2_sb[:, c, m * P:(m + 1) * P], top1[:, c],
                                          start=(c == 0), stop=(c == M1 // P - 1))
                mm.then_inc(top_acc, 1)
            for c in range(M2 // P):
                pe.wait_ge(top_relu, M1 // P + c + 1)
                mm = nc.tensor.matmul(top_banks[6][0:1], wt3_sb[:, c:c + 1], top2[:, c],
                                      start=(c == 0), stop=(c == M2 // P - 1))
            mm.then_inc(top_acc, 1)


def lay_out(np, inputs):
    tables = [np.asarray(inputs[f"tbl_{f}"]) for f in range(F)]
    ids = np.asarray(inputs["ids"])
    padded = np.zeros((NG * FPG, B), ids.dtype)
    padded[:F] = ids.T
    ids_laid = np.ascontiguousarray(padded.reshape(NG, FPG, NT, TB).transpose(1, 3, 2, 0).reshape(P, NT * NG))
    starts = np.zeros(NG * FPG, ids.dtype)
    starts[1:F] = np.cumsum([t.shape[0] for t in tables])[:F - 1]
    row_base = np.ascontiguousarray(np.repeat(starts.reshape(NG, FPG).T, TB, axis=0))
    w0 = np.asarray(inputs["L0_rec_W0"]).reshape(F, F, S)
    f = np.arange(F)
    w0a = np.zeros((C0 * SPC, F, S), w0.dtype)
    w0b = np.zeros((C0 * SPC, F, S), w0.dtype)
    for k in range(NSHIFT):
        w0a[k] = w0[f, (f + k) % F]
        if k:
            w0b[k] = w0[(f + k) % F, f]

    def chunks(w):
        return np.ascontiguousarray(w.reshape(C0, R0, S).transpose(1, 0, 2))

    parts = {True: [], False: []}
    for n in (1, 2):
        w = np.asarray(inputs[f"L0_rec_W{n}"])
        w = np.concatenate([w, np.zeros((C12 * P - F * H, S), w.dtype)]).reshape(C12, P, S)
        for u, kind in enumerate(KINDS[n]):
            parts[kind == WHOLE] += [w[c] for c in unit_chunks(n, u)]

    def by_partition(v):
        return np.ascontiguousarray(np.asarray(v).reshape(-1, P).T)

    return {
        "ids": ids_laid, "row_base": row_base, "tables": np.concatenate(tables, axis=0),
        "w0a": chunks(w0a), "w0b": chunks(w0b),
        "w12": np.stack(parts[True], axis=1), "w_splits": np.stack(parts[False], axis=1),
        "biases": by_partition(np.stack([np.asarray(inputs[f"L0_rec_b{n}"]) for n in range(3)])),
        "dense": np.ascontiguousarray(np.asarray(inputs["dense_ctx"]).T),
        "wt1": np.asarray(inputs["W_top1"]), "bt1": by_partition(inputs["b_top1"]),
        "wt2": np.asarray(inputs["W_top2"]), "bt2": by_partition(inputs["b_top2"]),
        "wt3": by_partition(inputs["W_top3"]),
    }


def kernel(**inputs):
    import numpy as np
    import concourse.bacc as bacc
    from concourse.bass_utils import run_bass_kernel_spmd

    nc = bacc.Bacc("TRN2", target_bir_lowering=False, num_devices=1)
    arrays, args = {}, []
    for name, a in lay_out(np, inputs).items():
        arrays[f"in_{name}"] = a
        args.append(nc.dram_tensor(f"in_{name}", a.shape, mybir.dt.from_np(a.dtype), kind="ExternalInput").ap())
    out = nc.dram_tensor("out_y", (B, 1), F32, kind="ExternalOutput").ap()
    build(nc, *args, out)
    r = run_bass_kernel_spmd(nc, [arrays], core_ids=[0])
    return r.results[0]["out_y"]
```

```python
from contextlib import ExitStack

import concourse.bass as bass
from concourse import mybir

F32 = mybir.dt.float32
F32R = mybir.dt.float32r
I32 = mybir.dt.int32
ALU = mybir.AluOpType
ACT = mybir.ActivationFunctionType
AX_X = mybir.AxisListType.X

P = 128
B = 512
F = 39
D = 16
S = 128
H = S // 2
TB = 32
COLS = TB * D
NT = B // TB
FPG = P // TB
NG = -(-F // FPG)
LASTG = (F - FPG * (NG - 1)) * TB
NSHIFT = (F + 1) // 2
SPC = P // F
R0 = SPC * F
C0 = -(-NSHIFT // SPC)
C12 = -(-F * H // P)
XROWS = F + C0 * SPC - 1
UNIT = 2
WHOLE, POOL, VECTOR = "whole", "pool", "vector"
KINDS = [
    [WHOLE, POOL, WHOLE, WHOLE],
    [POOL, VECTOR, WHOLE, POOL, VECTOR, POOL, WHOLE, POOL, VECTOR, WHOLE],
    [POOL, WHOLE, POOL, WHOLE, VECTOR, POOL, POOL, WHOLE, POOL, WHOLE],
]
ORDER = [
    [0, 2, 3, 1],
    [2, 1, 0, 4, 3, 6, 5, 9, 8, 7],
    [1, 0, 3, 2, 4, 7, 5, 6, 9, 8],
]
CHUNKS = [C0, C12, C12]
PROD_RING = 5
PART_RING = 4
GROUPS = [(0, 10, 2), (10, 14, 1), (14, 20, 1)]
FIRST = 4
GATHERS = [0, 1, 1, 1, 3, 1, 1, 0, 1, 1]
BEFORE_LOW = 3
WARM = (12, 14)
GATHER_AHEAD = 3
NDENSE = 16
M1, M2 = 512, 256
NTOP = M1 // P + M2 // P + 1
SECOND_AT, THIRD_AT, LATE_AT = 4, 6, 7
RELU1_AT = [1, 2, 3, 4]


def unit_chunks(layer, u):
    return range(UNIT * u, min(UNIT * (u + 1), CHUNKS[layer]))


def chunk_rows(layer, c):
    return min(R0, (NSHIFT - SPC * c) * F) if layer == 0 else min(P, F * H - P * c)


def weight_places():
    places = []
    for layer in range(3):
        at, whole, split = {}, 0, 0
        for u, kind in enumerate(KINDS[layer]):
            for c in unit_chunks(layer, u):
                if kind == WHOLE:
                    at[c], whole = whole, whole + 1
                else:
                    at[c], split = split, split + 1
        places.append((at, whole, split))
    return places


PLACES = weight_places()
W_WHOLE = [sum(PLACES[n][1] for n in range(m)) for m in range(4)]
W_SPLIT = [sum(PLACES[n][2] for n in range(m)) for m in range(4)]


class Counts:

    def __init__(self):
        self.nth = {}
        self.of_kind = {}
        self.split = {}
        self.used = {}
        self.prod_before = {}
        self.part_before = {}
        self.prod_slot, self.part_slot = {}, {}
        phases = [(0, 0)]
        for t in range(NT):
            phases += [(1, t)] + ([(0, t + 1)] if t + 1 < NT else []) + [(2, t)]
        ring_of = {}
        at = [0, 0]
        for layer, odd in [(1, 0), (0, 1), (2, 0), (1, 1), (0, 0), (2, 1)]:
            for u, kind in enumerate(KINDS[layer]):
                ring_of[layer, odd, u] = (at[0] % PROD_RING, at[1] % PART_RING)
                at[0] += kind != VECTOR
                at[1] += kind != WHOLE
        kinds = {WHOLE: 0, POOL: 0, VECTOR: 0}
        in_prod, in_part, splits = {}, {}, 0
        used = [0, 0]
        for layer, t in phases:
            for u, kind in enumerate(KINDS[layer]):
                key = (layer, t, u)
                self.nth[key] = len(self.nth)
                self.of_kind[key] = kinds[kind]
                kinds[kind] += 1
                prod, part = ring_of[layer, t % 2, u]
                if kind != VECTOR:
                    self.prod_slot[key], self.prod_before[key] = prod, in_prod.get(prod)
                    in_prod[prod] = key
                if kind != WHOLE:
                    self.part_slot[key], self.part_before[key] = part, in_part.get(part)
                    in_part[part] = key
                    self.split[key], splits = splits, splits + 1
            for u in ORDER[layer]:
                n = KINDS[layer][u] != WHOLE
                self.used[(layer, t, u)] = used[n]
                used[n] += 1


def build(nc, ids, row_base, tables, w0a, w0b, w12, w_splits, biases, dense, wt1, bt1, wt2, bt2, wt3, out):
    x_dram = nc.dram_tensor("x_rows", (NT, XROWS, COLS), F32)
    counts = Counts()

    with ExitStack() as ctx:
        def sb(name, shape, dt=F32):
            return ctx.enter_context(nc.sbuf_tensor(name, shape, dt))

        def psum(name, banks=1):
            return ctx.enter_context(nc.psum_tensor(name, [P, COLS] if banks == 1 else [P, banks, COLS], F32))

        def sem(name):
            return ctx.enter_context(nc.semaphore(name))

        ids_sb = sb("ids_sb", [P, NT * NG], I32)
        base_sb = sb("base_sb", [P, NG], I32)
        index = [sb(f"index{s}", [P, NG], I32) for s in range(2)]
        gathered = [sb(f"gathered{s}", [P, NG, D]) for s in range(2)]
        x_rep = [[sb(f"x_rep{g}_{s}", [P, hi - lo, COLS]) for s in range(n)] for g, (lo, hi, n) in enumerate(GROUPS)]
        x_shift = sb("x_shift", [P, C0, COLS])
        x_stack = sb("x_stack", [P, COLS])
        prod = sb("prod", [P, PROD_RING, UNIT, COLS])
        high = sb("high", [P, PART_RING, UNIT, COLS], F32R)
        low = sb("low", [P, PART_RING, UNIT, COLS], F32R)
        w0a_sb = sb("w0a_sb", [P, C0, S])
        w0b_sb = x_rep[0][1][:, 8:10].rearrange("p c n -> p (c n)")[:, 0:C0 * S].rearrange("p (c s) -> p c s", s=S)
        w_whole = sb("w_whole", [P, W_WHOLE[3] - W_WHOLE[1], S])
        w_high = sb("w_high", [P, W_SPLIT[3], S], F32R)
        w_low = sb("w_low", [P, W_SPLIT[3], S], F32R)
        NSPLIT = W_SPLIT[3] - W_SPLIT[1]
        w_raw = x_rep[0][1][:, 0:8].rearrange("p c n -> p (c n)")[:, 0:NSPLIT * S].rearrange("p (c s) -> p c s", s=S)
        bias = sb("bias", [P, 3])
        bias_t1 = sb("bias_t1", [P, M1 // P])
        bias_t2 = sb("bias_t2", [P, M2 // P])
        direct01 = sb("direct01", [P, COLS])
        direct2 = sb("direct2", [P, COLS])
        z01 = sb("z01", [P, B])
        z2 = sb("z2", [P, B])
        dense_sb = sb("dense_sb", [NDENSE, B])
        wt1_z = sb("wt1_z", [P, 2, M1])
        wt1_dense = sb("wt1_dense", [NDENSE, M1])
        wt2_sb = sb("wt2_sb", [P, M1 // P, M2])
        wt3_sb = sb("wt3_sb", [P, M2 // P])
        top1 = x_rep[0][0][:, 0:M1 // P]
        top2 = x_rep[0][0][:, M1 // P:(M1 + M2) // P]
        y_sb = sb("y_sb", [1, B])

        acc = [psum(f"acc{n}") for n in range(3)]
        x_ps = psum("x_ps")
        h_ps = [psum("h1_ps"), psum("h2_ps")]
        prod_ps = psum("prod_ps", UNIT)

        ids_in = sem("ids_in")
        w0_in = sem("w0_in")
        w_in = sem("w_in")
        w_raw_in = sem("w_raw_in")
        top_in = sem("top_in")
        bias_in = sem("bias_in")
        w0_summed = sem("w0_summed")
        w_high_ready = sem("w_high_ready")
        w_split = sem("w_split")
        index_ready = sem("index_ready")
        gather_done = [sem(f"gather_done{s}") for s in range(2)]
        rows_written = [sem(f"rows_written{s}") for s in range(2)]
        x_first_in = sem("x_first_in")
        x_rep_first_in = sem("x_rep_first_in")
        x_shift_in = sem("x_shift_in")
        x_stack_in = sem("x_stack_in")
        x_rep_in = [[sem(f"x_rep_in{g}_{s}") for s in range(n)] for g, (_, _, n) in enumerate(GROUPS)]
        x_ps_ready = sem("x_ps_ready")
        prod_ready = sem("prod_ready")
        high_ready = sem("high_ready")
        pool_low = sem("pool_low")
        vector_low = sem("vector_low")
        whole_used = sem("whole_used")
        split_used = sem("split_used")
        h_ready = [sem("h1_ready"), sem("h2_ready")]
        direct_ready = [sem(f"direct_ready{n}") for n in range(3)]
        z01_ready = sem("z01_ready")
        z2_ready = sem("z2_ready")
        top_acc = sem("top_acc")
        top_relu = sem("top_relu")
        y_ready = sem("y_ready")
        y_out = sem("y_out")

        def at(f, tile):
            t, i = tile
            return f(t) if i is None else i * (f(t + 2) - f(t)) + f(t)

        def multiplied(layer, tile, u=-1):
            u = u % len(KINDS[layer])
            return at(lambda t: counts.nth[layer, t, u] + 1, tile)

        def contracted(layer, tile, u=None):
            u = ORDER[layer][-1] if u is None else u
            kind = KINDS[layer][u]
            return (whole_used if kind == WHOLE else split_used), at(lambda t: counts.used[layer, t, u] + 1, tile)

        def parts_free(eng, layer, tile, u):
            before = counts.part_before[layer, tile[0], u]
            if before:
                eng.wait_ge(*contracted(before[0], (before[1], tile[1]), before[2]))

        def run_tiles(eng, tile, peeled=2):
            for t in range(2):
                tile((t, None))
            with eng.Fori(0, (NT - 2 - peeled) // 2) as i:
                for s in range(2):
                    tile((2 + s, i))
            for t in range(NT - peeled, NT):
                tile((t, None))

        def ahead(tile, n=1):
            return tile[0] + n, tile[1]

        w0_split = [(PLACES[0][0][c], c) for u, kind in enumerate(KINDS[0]) if kind != WHOLE for c in unit_chunks(0, u)]

        def top_bank(m):
            return [acc[0], x_ps, h_ps[0], acc[1]][m % 4]

        EARLY, LATE = slice(0, (NT - 1) * TB), slice((NT - 1) * TB, NT * TB)

        block = ctx.enter_context(nc.Block())

        @block.gpsimd
        def _(pool):
            def make_index(t, s):
                nc.gpsimd.tensor_tensor(index[s][:], ids_sb[:, bass.ds(t * NG, NG)], base_sb[:],
                                        ALU.add).then_inc(index_ready, 1)

            def gather(s, js):
                for j in js:
                    n = P if j < NG - 1 else LASTG
                    nc.gpsimd.indirect_dma_start(
                        gathered[s][0:n, j, :], None, tables[:, :],
                        bass.IndirectOffsetOnAxis(ap=index[s][0:n, j:j + 1], axis=0),
                    ).then_inc(gather_done[s], 16)

            def low_part(layer, tile, u):
                pool.wait_ge(high_ready, at(lambda t: counts.split[layer, t, u] + 1, tile))
                key = (layer, tile[0], u)
                n, rows = len(unit_chunks(layer, u)), R0 if layer == 0 else P
                ring, part = counts.prod_slot[key], counts.part_slot[key]
                nc.gpsimd.tensor_tensor(low[0:rows, part, 0:n], prod[0:rows, ring, 0:n],
                                        high[0:rows, part, 0:n].bitcast(F32), ALU.subtract).then_inc(pool_low, 1)

            def tile(tl):
                t, i = tl
                s = (t + 1) % 2
                units = [(n, ahead(tl) if n == 0 else tl, u) for n in (1, 0, 2)
                         for u, kind in enumerate(KINDS[n]) if kind == POOL and (n or t + 1 < NT)]
                more = t + GATHER_AHEAD < NT
                if more:
                    pool.wait_ge(rows_written[s], at(lambda t: (t + 1) // 2 * 48 + 48, tl))
                    ahead_t = t + GATHER_AHEAD
                    make_index(ahead_t if i is None else i * 2 + ahead_t, s)
                    pool.wait_ge(index_ready, at(lambda t: t + GATHER_AHEAD + 1, tl))
                for k, (layer, tile_, u) in enumerate(units):
                    low_part(layer, tile_, u)
                    if more:
                        gather(s, range(sum(GATHERS[:k]), sum(GATHERS[:k + 1])))

            pool.wait_ge(ids_in, 32)
            for t in range(GATHER_AHEAD):
                if t >= 2:
                    pool.wait_ge(rows_written[t % 2], 48)
                make_index(t, t % 2)
                pool.wait_ge(index_ready, t + 1)
                last = t == GATHER_AHEAD - 1
                gather(t % 2, range(BEFORE_LOW if last else NG))
                if last:
                    for u, kind in enumerate(KINDS[0]):
                        if kind == POOL:
                            low_part(0, (0, None), u)
                    gather(t % 2, range(BEFORE_LOW, NG))
            run_tiles(pool, tile, peeled=GATHER_AHEAD + 1)

        @block.sync
        def _(sp):
            def write_rows(t):
                s = t % 2
                sp.wait_ge(gather_done[s], (t // 2 + 1) * (16 * NG))
                full = FPG * (NG - 1)
                again = -(-(XROWS - F) // FPG)
                rows = x_dram[t]
                sp.dma_start(rows[0:full].rearrange("(j f) (b d) -> (f b) j d", f=FPG, d=D),
                             gathered[s][:, 0:NG - 1, :]).then_inc(rows_written[s], 16)
                sp.dma_start(rows[full:F].rearrange("f (b d) -> (f b) d", d=D),
                             gathered[s][0:LASTG, NG - 1, :]).then_inc(rows_written[s], 16)
                sp.dma_start(rows[F:F + again * FPG].rearrange("(j f) (b d) -> (f b) j d", f=FPG, d=D),
                             gathered[s][:, 0:again, :]).then_inc(rows_written[s], 16)

            def rows_are_written(t):
                sp.wait_ge(rows_written[t % 2], (t // 2 + 1) * 48)

            def load_layer0(t):
                if t:
                    sp.wait_ge(prod_ready, multiplied(0, (t - 1, None)))
                sp.dma_start(x_stack[0:R0],
                             bass.AP(x_dram, t * (XROWS * COLS), [[0, SPC], [COLS, F], [1, COLS]])
                             ).then_inc(x_stack_in, 16)
                for lo, hi in [(0, FIRST), (FIRST, C0)] if t == 0 else [(0, C0)]:
                    for k in range(SPC):
                        sp.dma_start(x_shift[k * F:(k + 1) * F, lo:hi],
                                     bass.AP(x_dram, (t * XROWS + k + SPC * lo) * COLS,
                                             [[COLS, F], [SPC * COLS, hi - lo], [1, COLS]])
                                     ).then_inc(x_first_in if hi < C0 else x_shift_in, 16)

            def load_rep(t, g):
                lo, hi, n = GROUPS[g]
                if t == 1 and n == 2:
                    sp.wait_ge(w_split, W_SPLIT[1] + 1)
                elif t >= n:
                    sp.wait_ge(prod_ready, multiplied(2, (t - n, None), (hi - 1) // UNIT))
                for a, b in [(lo, FIRST), (FIRST, hi)] if (t, g) == (0, 0) else [(lo, hi)]:
                    for half in range(2):
                        sp.dma_start(x_rep[g][t % n][half * H:(half + 1) * H, a - lo:b - lo],
                                     bass.AP(x_dram, (t * XROWS + (2 * a + half)) * COLS,
                                             [[0, H], [2 * COLS, b - a], [1, COLS]])
                                     ).then_inc(x_rep_first_in if b == FIRST else x_rep_in[g][t % n], 16)

            sp.dma_start(ids_sb[:], ids).then_inc(ids_in, 16)
            sp.dma_start(base_sb[:], row_base).then_inc(ids_in, 16)
            sp.dma_start(w0a_sb[0:R0], w0a).then_inc(w0_in, 16)
            sp.dma_start(w0b_sb[0:R0], w0b).then_inc(w0_in, 16)
            sp.dma_start(bias[:], biases).then_inc(bias_in, 16)
            sp.dma_start(w_whole[:], w12).then_inc(w_in, 16)
            sp.dma_start(w_raw, w_splits).then_inc(w_raw_in, 16)
            write_rows(0)
            rows_are_written(0)
            load_layer0(0)
            load_rep(0, 0)
            write_rows(1)
            for g in range(1, len(GROUPS)):
                load_rep(0, g)
            for dst, src in (
                (wt1_z[:], wt1[0:2 * P].rearrange("(c p) n -> p c n", p=P)),
                (wt1_dense[:], wt1[2 * P:2 * P + NDENSE]), (dense_sb[:], dense),
                (wt2_sb[:], wt2.rearrange("(c p) n -> p c n", p=P)),
                (wt3_sb[:], wt3), (bias_t1[:], bt1), (bias_t2[:], bt2),
            ):
                sp.dma_start(dst, src).then_inc(top_in, 16)
            for t in range(1, NT):
                rows_are_written(t)
                load_layer0(t)
                load_rep(t, 0)
                if t + 1 < NT:
                    write_rows(t + 1)
                for g in range(1, len(GROUPS)):
                    load_rep(t, g)
            sp.wait_ge(y_ready, 2)
            sp.dma_start(out.rearrange("b a -> a b"), y_sb[:]).then_inc(y_out, 16)
            sp.wait_ge(y_out, 16)

        @block.vector
        def _(dve):
            def multiply(layer, tile, u):
                key = (layer, tile[0], u)
                n, rows = len(unit_chunks(layer, u)), R0 if layer == 0 else P
                c = UNIT * u
                if layer == 0:
                    if tile == (0, None) and c == FIRST:
                        dve.wait_ge(x_shift_in, 16 * SPC)
                    x, h = x_shift[0:rows, c:c + n], x_ps
                else:
                    g = next(k for k, (lo, hi, _) in enumerate(GROUPS) if lo <= c < hi)
                    lo, _, buffers = GROUPS[g]
                    in_parts = (layer, tile, g) == (1, (0, None), 0)
                    if in_parts and c == lo:
                        dve.wait_ge(x_rep_first_in, 32)
                    if c == (FIRST if in_parts else lo):
                        s = tile[0] % buffers
                        dve.wait_ge(x_rep_in[g][s], at(lambda t: (t // buffers + 1) * 32, tile))
                    x, h = x_rep[g][tile[0] % buffers][:, c - lo:c - lo + n], h_ps[layer - 1]
                if KINDS[layer][u] == VECTOR:
                    if counts.of_kind[key]:
                        dve.wait_ge(vector_low, at(lambda t: counts.of_kind[layer, t, u], tile))
                    to = prod_ps[0:rows, 0:n]
                else:
                    before = counts.prod_before[key]
                    if before:
                        b, of = (before[1], tile[1]), KINDS[before[0]][before[2]]
                        if of == WHOLE:
                            dve.wait_ge(*contracted(before[0], b, before[2]))
                        else:
                            dve.wait_ge(pool_low, at(lambda t: counts.of_kind[before[0], t, before[2]] + 1, b))
                    to = prod[0:rows, counts.prod_slot[key], 0:n]
                nc.vector.tensor_tensor(to, x, bass.AP(h, 0, [[COLS, rows], [0, n], [1, COLS]]),
                                        ALU.mult).then_inc(prod_ready, 1)

            def low_part(layer, tile, u):
                dve.wait_ge(high_ready, at(lambda t: counts.split[layer, t, u] + 1, tile))
                n, rows = len(unit_chunks(layer, u)), R0 if layer == 0 else P
                part = counts.part_slot[layer, tile[0], u]
                nc.vector.tensor_tensor(low[0:rows, part, 0:n], prod_ps[0:rows, 0:n],
                                        high[0:rows, part, 0:n].bitcast(F32), ALU.subtract).then_inc(vector_low, 1)

            def layer(n, tile, extra=None):
                waiting = None
                for u, kind in enumerate(KINDS[n]):
                    multiply(n, tile, u)
                    if waiting is not None:
                        low_part(n, tile, waiting)
                    waiting = u if kind == VECTOR else None
                    if extra and u == extra[0]:
                        extra[1]()

            def sum_dims(z, z_in, direct, count, done, tile):
                dve.wait_ge(z_in, at(count, tile))
                t, i = tile
                cols = bass.ds(t * TB if i is None else i * (2 * TB) + t * TB, TB)
                nc.vector.tensor_reduce(z[:, cols], direct[:].rearrange("p (b d) -> p b d", d=D),
                                        AX_X, ALU.add).then_inc(done, 1)

            def sum01(tile):
                sum_dims(z01, direct_ready[1], direct01, lambda t: t + 1, z01_ready, tile)

            def sum2(tile):
                sum_dims(z2, direct_ready[2], direct2, lambda t: t + 1, z2_ready, tile)

            def tile(tl):
                dve.wait_ge(h_ready[0], at(lambda t: 2 * t + 2, tl))
                layer(1, tl, (5, lambda: sum2(ahead(tl, -1))) if tl[0] else None)
                if tl[0] + 1 < NT:
                    nxt = ahead(tl)
                    dve.wait_ge(x_ps_ready, at(lambda t: t + 1, nxt))
                    dve.wait_ge(x_shift_in, at(lambda t: (t + 1) * (16 * SPC), nxt))
                    layer(0, nxt)
                dve.wait_ge(h_ready[1], at(lambda t: 2 * t + 2, tl))
                layer(2, tl, (4, lambda: sum01(tl)))

            dve.wait_ge(w0_in, 32)
            nc.vector.tensor_tensor(w0a_sb[0:R0], w0a_sb[0:R0], w0b_sb[0:R0], ALU.add).then_inc(w0_summed, 1)
            k = W_SPLIT[1]
            dve.wait_ge(w_high_ready, k + 1)
            for at_, c in w0_split:
                nc.vector.tensor_tensor(w_low[0:R0, at_], w0a_sb[0:R0, c], w_high[0:R0, at_].bitcast(F32),
                                        ALU.subtract).then_inc(w_split, 1)
            nc.vector.tensor_tensor(w_low[:, k:], w_raw, w_high[:, k:].bitcast(F32),
                                    ALU.subtract).then_inc(w_split, 1)
            dve.wait_ge(x_ps_ready, 1)
            dve.wait_ge(x_first_in, 16 * SPC)
            layer(0, (0, None))
            run_tiles(dve, tile)
            sum2((NT - 1, None))

        @block.scalar
        def _(act):
            def stack(tile):
                act.wait_ge(x_stack_in, at(lambda t: (t + 1) * 16, tile))
                nc.scalar.copy(x_ps[0:R0], x_stack[0:R0]).then_inc(x_ps_ready, 1)

            def high_part(layer, tile, u):
                kind, key = KINDS[layer][u], (layer, tile[0], u)
                if kind == WHOLE:
                    return
                parts_free(act, layer, tile, u)
                act.wait_ge(prod_ready, multiplied(layer, tile, u))
                n, rows = len(unit_chunks(layer, u)), R0 if layer == 0 else P
                src = prod_ps[0:rows, 0:n] if kind == VECTOR else prod[0:rows, counts.prod_slot[key], 0:n]
                nc.scalar.copy(high[0:rows, counts.part_slot[key], 0:n], src).then_inc(high_ready, 1)

            def layer(n, tile, extra):
                for u in range(len(KINDS[n])):
                    high_part(n, tile, u)
                    if u in extra:
                        extra[u]()

            def outputs(n, tile):
                act.wait_ge(*contracted(n, tile))
                if n == 2:
                    nc.scalar.activation(direct2[:], acc[2][:], ACT.Relu, bias=bias[:, 2:3]).then_inc(direct_ready[2], 1)
                    return
                for half in range(2):
                    nc.scalar.activation(h_ps[n][half * H:(half + 1) * H], acc[n][0:H], ACT.Relu,
                                         bias=bias[0:H, n:n + 1]).then_inc(h_ready[n], 1)
                if n == 0 and tile[0]:
                    act.wait_ge(z01_ready, at(lambda t: t, tile))
                nc.scalar.activation(direct01[n * H:(n + 1) * H], acc[n][H:P], ACT.Relu,
                                     bias=bias[H:P, n:n + 1]).then_inc(direct_ready[n], 1)

            def tile(tl):
                t = tl[0]
                more = t + 1 < NT
                extra = {}
                if t:
                    extra[4] = lambda: outputs(2, ahead(tl, -1))
                if more:
                    extra[7] = lambda: stack(ahead(tl))
                layer(1, tl, extra)
                if more:
                    layer(0, ahead(tl), {})
                outputs(1, tl)
                if more:
                    layer(2, tl, {7: lambda: outputs(0, ahead(tl))})

            def top_output(m, cols):
                act.wait_ge(top_acc, m + 1 + (0 if cols == EARLY else NTOP))
                if m < M1 // P:
                    nc.scalar.activation(top1[:, m, cols], top_bank(m)[:, cols], ACT.Relu,
                                         bias=bias_t1[:, m:m + 1]).then_inc(top_relu, 1)
                elif m < NTOP - 1:
                    k = m - M1 // P
                    nc.scalar.activation(top2[:, k, cols], top_bank(k)[:, cols], ACT.Relu,
                                         bias=bias_t2[:, k:k + 1]).then_inc(top_relu, 1)
                else:
                    nc.scalar.copy(y_sb[:, cols], top_bank(2)[0:1, cols]).then_inc(y_ready, 1)

            act.wait_ge(w0_summed, 1)
            k = W_SPLIT[1]
            for at_, c in w0_split:
                nc.scalar.copy(w_high[0:R0, at_], w0a_sb[0:R0, c]).then_inc(w_high_ready, 1)
            act.wait_ge(w_raw_in, 16)
            nc.scalar.copy(w_high[:, k:], w_raw).then_inc(w_high_ready, 1)
            stack((0, None))
            layer(0, (0, None), {})
            act.wait_ge(bias_in, 16)
            outputs(0, (0, None))
            run_tiles(act, tile)
            act.wait_ge(top_in, 16 * 7)
            layer(2, (NT - 1, None), {RELU1_AT[m]: lambda m=m: top_output(m, EARLY) for m in range(M1 // P)})
            for m in range(M1 // P, NTOP):
                top_output(m, EARLY)
            outputs(2, (NT - 1, None))
            for m in range(NTOP):
                top_output(m, LATE)

        @block.tensor
        def _(pe):
            def contract(layer, tile, extra={}):
                place, _, _ = PLACES[layer]
                first = True
                for nth, u in enumerate(ORDER[layer]):
                    if nth in extra:
                        extra[nth]()
                    kind, key = KINDS[layer][u], (layer, tile[0], u)
                    if kind == WHOLE:
                        pe.wait_ge(prod_ready, multiplied(layer, tile, u))
                    else:
                        pe.wait_ge(pool_low if kind == POOL else vector_low,
                                   at(lambda t: counts.of_kind[layer, t, u] + 1, tile))
                    for k, c in enumerate(unit_chunks(layer, u)):
                        rows = chunk_rows(layer, c)
                        last = u == ORDER[layer][-1] and c == unit_chunks(layer, u)[-1]
                        if kind == WHOLE:
                            w = w0a_sb[0:rows, c] if layer == 0 else w_whole[0:rows, W_WHOLE[layer] - W_WHOLE[1] + place[c]]
                            pairs = [(w, prod[0:rows, counts.prod_slot[key], k])]
                        else:
                            n, part = W_SPLIT[layer] + place[c], counts.part_slot[key]
                            hi, lo = w_high[0:rows, n], w_low[0:rows, n]
                            pairs = [(hi, low[0:rows, part, k]), (hi, high[0:rows, part, k]), (lo, high[0:rows, part, k])]
                        for m, (w, p) in enumerate(pairs):
                            mm = nc.tensor.matmul(acc[layer][:], w, p, start=first,
                                                  stop=last and m == len(pairs) - 1)
                            first = False
                    mm.then_inc(whole_used if kind == WHOLE else split_used, 1)

            def tile(tl):
                contract(1, tl)
                if tl[0] + 1 < NT:
                    pe.wait_ge(direct_ready[0], at(lambda t: t + 1, tl))
                    contract(0, ahead(tl))
                    contract(2, tl)

            def keep_warm(n):
                some = w_high[:, W_SPLIT[1]:W_SPLIT[1] + COLS // S]
                for _ in range(n):
                    nc.tensor.matmul(acc[2][:], w_high[:, W_SPLIT[1]], some, start=True, stop=True)

            def top_first(cols, parts):
                operands = {"dense": (wt1_dense, dense_sb), "z01": (wt1_z[:, 0], z01), "z2": (wt1_z[:, 1], z2)}
                for m in range(M1 // P):
                    if cols == EARLY:
                        pe.wait_ge(direct_ready[0 if m < 3 else 1], NT)
                    for part in parts:
                        w, z = operands[part]
                        mm = nc.tensor.matmul(top_bank(m)[:, cols], w[:, m * P:(m + 1) * P], z[:, cols],
                                              start=part == "dense", stop=part == "z2")
                    if "z2" in parts:
                        mm.then_inc(top_acc, 1)

            def top_second(cols):
                relus = 0 if cols == EARLY else NTOP - 1
                for m in range(M2 // P):
                    for c in range(M1 // P):
                        if m == 0:
                            pe.wait_ge(top_relu, relus + c + 1)
                        mm = nc.tensor.matmul(top_bank(m)[:, cols], wt2_sb[:, c, m * P:(m + 1) * P], top1[:, c, cols],
                                              start=(c == 0), stop=(c == M1 // P - 1))
                    mm.then_inc(top_acc, 1)

            def top_third(cols):
                relus = M1 // P + (0 if cols == EARLY else NTOP - 1)
                for c in range(M2 // P):
                    pe.wait_ge(top_relu, relus + c + 1)
                    mm = nc.tensor.matmul(top_bank(2)[0:1, cols], wt3_sb[:, c:c + 1], top2[:, c, cols],
                                          start=(c == 0), stop=(c == M2 // P - 1))
                mm.then_inc(top_acc, 1)

            def late_first():
                pe.wait_ge(y_ready, 1)
                pe.wait_ge(z01_ready, NT)
                top_first(LATE, ["dense", "z01"])

            pe.wait_ge(w0_summed, 1)
            pe.wait_ge(w_split, W_SPLIT[1] + 1)
            pe.wait_ge(rows_written[0], 48)
            keep_warm(WARM[0])
            contract(0, (0, None))
            keep_warm(WARM[1])
            pe.wait_ge(w_in, 16)
            run_tiles(pe, tile)
            last = (NT - 1, None)
            pe.wait_ge(top_in, 16 * 7)
            pe.wait_ge(z01_ready, NT - 1)
            pe.wait_ge(z2_ready, NT - 1)
            top_first(EARLY, ["dense", "z01", "z2"])
            contract(2, last, {SECOND_AT: lambda: top_second(EARLY), THIRD_AT: lambda: top_third(EARLY),
                               LATE_AT: late_first})
            pe.wait_ge(z2_ready, NT)
            top_first(LATE, ["z2"])
            top_second(LATE)
            top_third(LATE)


def lay_out(np, inputs):
    tables = [np.asarray(inputs[f"tbl_{f}"]) for f in range(F)]
    ids = np.asarray(inputs["ids"])
    padded = np.zeros((NG * FPG, B), ids.dtype)
    padded[:F] = ids.T
    ids_laid = np.ascontiguousarray(padded.reshape(NG, FPG, NT, TB).transpose(1, 3, 2, 0).reshape(P, NT * NG))
    starts = np.zeros(NG * FPG, ids.dtype)
    starts[1:F] = np.cumsum([t.shape[0] for t in tables])[:F - 1]
    row_base = np.ascontiguousarray(np.repeat(starts.reshape(NG, FPG).T, TB, axis=0))
    w0 = np.asarray(inputs["L0_rec_W0"]).reshape(F, F, S)
    f = np.arange(F)
    w0a = np.zeros((C0 * SPC, F, S), w0.dtype)
    w0b = np.zeros((C0 * SPC, F, S), w0.dtype)
    for k in range(NSHIFT):
        w0a[k] = w0[f, (f + k) % F]
        if k:
            w0b[k] = w0[(f + k) % F, f]

    def chunks(w):
        return np.ascontiguousarray(w.reshape(C0, R0, S).transpose(1, 0, 2))

    parts = {True: [], False: []}
    for n in (1, 2):
        w = np.asarray(inputs[f"L0_rec_W{n}"])
        w = np.concatenate([w, np.zeros((C12 * P - F * H, S), w.dtype)]).reshape(C12, P, S)
        for u, kind in enumerate(KINDS[n]):
            parts[kind == WHOLE] += [w[c] for c in unit_chunks(n, u)]

    def by_partition(v):
        return np.ascontiguousarray(np.asarray(v).reshape(-1, P).T)

    return {
        "ids": ids_laid, "row_base": row_base, "tables": np.concatenate(tables, axis=0),
        "w0a": chunks(w0a), "w0b": chunks(w0b),
        "w12": np.stack(parts[True], axis=1), "w_splits": np.stack(parts[False], axis=1),
        "biases": by_partition(np.stack([np.asarray(inputs[f"L0_rec_b{n}"]) for n in range(3)])),
        "dense": np.ascontiguousarray(np.asarray(inputs["dense_ctx"]).T),
        "wt1": np.asarray(inputs["W_top1"]), "bt1": by_partition(inputs["b_top1"]),
        "wt2": np.asarray(inputs["W_top2"]), "bt2": by_partition(inputs["b_top2"]),
        "wt3": by_partition(inputs["W_top3"]),
    }


def kernel(**inputs):
    import numpy as np
    import concourse.bacc as bacc
    from concourse.bass_utils import run_bass_kernel_spmd

    nc = bacc.Bacc("TRN2", target_bir_lowering=False, num_devices=1)
    arrays, args = {}, []
    for name, a in lay_out(np, inputs).items():
        arrays[f"in_{name}"] = a
        args.append(nc.dram_tensor(f"in_{name}", a.shape, mybir.dt.from_np(a.dtype), kind="ExternalInput").ap())
    out = nc.dram_tensor("out_y", (B, 1), F32, kind="ExternalOutput").ap()
    build(nc, *args, out)
    r = run_bass_kernel_spmd(nc, [arrays], core_ids=[0])
    return r.results[0]["out_y"]
```
